# Optimizing a Trainium2 kernel written in Bass

```python
import numpy as np
import jax
import jax.numpy as jnp

def _softmax(x, axis=-1):
    return jax.nn.softmax(x, axis=axis)

def _gelu(x):
    return jax.nn.gelu(x, approximate=True)

def _silu(x):
    return jax.nn.silu(x)

def _sigmoid(x):
    return jax.nn.sigmoid(x)

def _layernorm(x, axis=-1, eps=1e-05):
    m = jnp.mean(x, axis=axis, keepdims=True)
    v = jnp.var(x, axis=axis, keepdims=True)
    return (x - m) / jnp.sqrt(v + eps)

def _scatter_add(tgt, idx, src, axis=0):
    return tgt.at[idx].add(src)

def _segment_sum(src, seg, n):
    return jax.ops.segment_sum(src, seg, n)
kernel_name = 'mk_cond_resid_d2_seqx_r4_7d1b5f'

def setup_inputs(seed: int=0):
    np.random.seed(seed)
    _w = jnp.asarray

    def _rec_inputs():
        import jax
        import jax.numpy as jnp
        _rk = jax.random.key(seed)
        x = 7.22e-05 + 1 * jax.random.normal(jax.random.fold_in(_rk, 1), (32, 256, 256), jnp.float32)
        _lenS = 256 - jax.random.randint(jax.random.fold_in(_rk, 7), (32,), 0, max(1, 256 // 4) + 1, jnp.int32)
        _lenS2 = 256 - jax.random.randint(jax.random.fold_in(_rk, 8), (32,), 0, max(1, 256 // 4) + 1, jnp.int32)
        fside_BxSxS_0 = 4.13588e-05 + 0.999923 * jax.random.normal(jax.random.fold_in(_rk, 11), (32, 256, 256), jnp.float32)
        itok_B_0_5 = jax.random.randint(jax.random.fold_in(_rk, 12), (32,), 0, 6, jnp.int32)
        condB_tauraws = -5.74692 + 0.777674 * jax.random.normal(jax.random.fold_in(_rk, 13), (32,), jnp.float32)
        cond_256 = -0.000235209 + 0.019331 * jax.random.normal(jax.random.fold_in(_rk, 14), (32, 64), jnp.float32)
        condB_bn2 = jnp.zeros((32,), jnp.float32)
        cond_1024 = -4.10585e-05 + 0.0199478 * jax.random.normal(jax.random.fold_in(_rk, 16), (32, 256), jnp.float32)
        return (x, fside_BxSxS_0, itok_B_0_5, condB_tauraws, cond_256, condB_bn2, cond_1024)
    x, fside_BxSxS_0, itok_B_0_5, condB_tauraws, cond_256, condB_bn2, cond_1024 = _rec_inputs()

    def _L0_cond_setup():
        import jax, jax.numpy as jnp
        import numpy as np
        B, S, D = (8, 256, 256)
        NUM_STAGES = 6
        key = jax.random.key(seed)
        k1, k2, k3, k4, k5 = jax.random.split(key, 5)
        return {'query': jax.random.normal(k1, (B, S, D), dtype=jnp.float32), 'key': jax.random.normal(k2, (B, S, D), dtype=jnp.float32), 'value': jax.random.normal(k3, (B, S, D), dtype=jnp.float32), 'braak_embed': jax.random.normal(k4, (NUM_STAGES, D), dtype=jnp.float32), 'braak_stages': jax.random.randint(k5, (B,), 0, NUM_STAGES, dtype=jnp.int64)}
    _L0_cond_all = _L0_cond_setup()
    _L0_cond_in = {k: v for k, v in _L0_cond_all.items() if k in ('braak_embed',)}
    del _L0_cond_all

    def _L1_cond_setup():
        import jax, jax.numpy as jnp
        import numpy as np
        import math
        B, T, E, D = (4, 512, 256, 4)

        def _tau_init(t):
            a = 0.1 ** (1.0 / max(t - 1, 1))
            tt = -math.log(max(a, 1e-10))
            return math.log(math.exp(tt) - 1 + 1e-10)

        def causal_ema(b, tau_raw):
            alpha = jnp.exp(-jax.nn.softplus(tau_raw)).astype(b.dtype)

            def step(h, bt):
                h = alpha * h + bt
                return (h, h)
            h0 = jnp.zeros((b.shape[0], b.shape[2]), b.dtype)
            _, hs = jax.lax.scan(step, h0, jnp.swapaxes(b, 0, 1))
            return jnp.swapaxes(hs, 0, 1)
        key = jax.random.key(seed)
        ks = jax.random.split(key, 10)
        s = 0.02
        return {'x': jax.random.normal(ks[0], (B, T, E), jnp.float32), 'tau_ctx': jnp.float32(_tau_init(max(T // 2, 4))), 'tau_raws': jnp.array([_tau_init(max(T // 2 ** i, 2)) for i in range(D)], jnp.float32), 'Wg': jax.random.normal(ks[1], (E, 2 * E), jnp.float32) * s, 'bg': jnp.full((E,), -0.5, jnp.float32), 'Wn1': jax.random.normal(ks[2], (E // 4, E), jnp.float32) * s, 'bn1': jnp.zeros((E // 4,), jnp.float32), 'Wn2': jax.random.normal(ks[3], (D, E // 4), jnp.float32) * s, 'bn2': jnp.zeros((D,), jnp.float32), 'blend': jax.random.normal(ks[4], (D, E), jnp.float32) * s, 'Wsoma': jax.random.normal(ks[5], (E, E), jnp.float32) * s, 'bsoma': jnp.zeros((E,), jnp.float32), 'Wtemp': jax.random.normal(ks[6], (E, E), jnp.float32) * s, 'btemp': jnp.zeros((E,), jnp.float32), 'Wout': jax.random.normal(ks[7], (E, E), jnp.float32) * s, 'gamma': jnp.ones((E,), jnp.float32), 'beta': jnp.zeros((E,), jnp.float32)}
    _L1_cond_all = _L1_cond_setup()
    _L1_cond_in = {k: v for k, v in _L1_cond_all.items() if k in ('tau_ctx', 'Wg', 'bg', 'Wn1', 'bn1', 'Wsoma', 'bsoma', 'Wtemp', 'btemp', 'Wout', 'gamma', 'beta')}
    del _L1_cond_all
    return {'x': x, 'fside_BxSxS_0': fside_BxSxS_0, 'itok_B_0_5': itok_B_0_5, 'condB_tauraws': condB_tauraws, 'cond_256': cond_256, 'condB_bn2': condB_bn2, 'cond_1024': cond_1024, 'L0_cond_braak_embed': _L0_cond_in['braak_embed'], 'L1_cond_tau_ctx': _L1_cond_in['tau_ctx'], 'L1_cond_Wg': _L1_cond_in['Wg'], 'L1_cond_bg': _L1_cond_in['bg'], 'L1_cond_Wn1': _L1_cond_in['Wn1'], 'L1_cond_bn1': _L1_cond_in['bn1'], 'L1_cond_Wsoma': _L1_cond_in['Wsoma'], 'L1_cond_bsoma': _L1_cond_in['bsoma'], 'L1_cond_Wtemp': _L1_cond_in['Wtemp'], 'L1_cond_btemp': _L1_cond_in['btemp'], 'L1_cond_Wout': _L1_cond_in['Wout'], 'L1_cond_gamma': _L1_cond_in['gamma'], 'L1_cond_beta': _L1_cond_in['beta']}

def reference(x, fside_BxSxS_0, itok_B_0_5, condB_tauraws, cond_256, condB_bn2, cond_1024, L0_cond_braak_embed, L1_cond_tau_ctx, L1_cond_Wg, L1_cond_bg, L1_cond_Wn1, L1_cond_bn1, L1_cond_Wsoma, L1_cond_bsoma, L1_cond_Wtemp, L1_cond_btemp, L1_cond_Wout, L1_cond_gamma, L1_cond_beta):
    import jax
    import jax.numpy as jnp

    def _L0_cond_ref(query, key, value, braak_embed, braak_stages):
        import jax, jax.numpy as jnp
        import numpy as np
        B, S, D = (8, 256, 256)
        NUM_STAGES = 6
        bias = braak_embed[braak_stages][..., None]
        q = query + bias
        attn = jnp.einsum('bsd,btd->bst', q, key)
        attn = jax.nn.softmax(attn, axis=-1)
        return jnp.einsum('bst,btd->bsd', attn, value)

    def _L1_cond_ref(x, tau_ctx, tau_raws, Wg, bg, Wn1, bn1, Wn2, bn2, blend, Wsoma, bsoma, Wtemp, btemp, Wout, gamma, beta):
        import jax, jax.numpy as jnp
        import numpy as np
        import math
        B, T, E, D = (4, 512, 256, 4)

        def _tau_init(t):
            a = 0.1 ** (1.0 / max(t - 1, 1))
            tt = -math.log(max(a, 1e-10))
            return math.log(math.exp(tt) - 1 + 1e-10)

        def causal_ema(b, tau_raw):
            alpha = jnp.exp(-jax.nn.softplus(tau_raw)).astype(b.dtype)

            def step(h, bt):
                h = alpha * h + bt
                return (h, h)
            h0 = jnp.zeros((b.shape[0], b.shape[2]), b.dtype)
            _, hs = jax.lax.scan(step, h0, jnp.swapaxes(b, 0, 1))
            return jnp.swapaxes(hs, 0, 1)
        ctx = causal_ema(x, tau_ctx)
        gate_in = jnp.concatenate([x, ctx], axis=-1)
        wg = jax.nn.sigmoid(jnp.einsum('btc,ec->bte', gate_in, Wg) + bg)
        gated = x * wg
        h1 = jax.nn.gelu(jnp.einsum('btc,hc->bth', x, Wn1) + bn1, approximate=False)
        mod = 0.5 + jax.nn.sigmoid(jnp.einsum('bth,dh->btd', h1, Wn2) + bn2)
        traces = jax.vmap(lambda tau, m: causal_ema(gated * m[..., None], tau))(tau_raws, jnp.moveaxis(mod, -1, 0))
        blend_w = jax.nn.softmax(blend, axis=0)
        temporal = jnp.einsum('dbtc,dc->btc', traces, blend_w)
        gate = jax.nn.sigmoid(jnp.einsum('btc,ec->bte', temporal, Wtemp) + btemp)
        soma = jax.nn.gelu(jnp.einsum('btc,ec->bte', x, Wsoma) + bsoma, approximate=False)
        out = jnp.einsum('btc,ec->bte', soma * gate, Wout)
        mu = out.mean(-1, keepdims=True)
        var = out.var(-1, keepdims=True)
        return (out - mu) / jnp.sqrt(var + 1e-05) * gamma + beta
    x = x + _L0_cond_ref(x, fside_BxSxS_0, fside_BxSxS_0, L0_cond_braak_embed, itok_B_0_5)
    x = x + _L1_cond_ref(x, L1_cond_tau_ctx, condB_tauraws, L1_cond_Wg, L1_cond_bg, L1_cond_Wn1, L1_cond_bn1, cond_256, condB_bn2, cond_1024, L1_cond_Wsoma, L1_cond_bsoma, L1_cond_Wtemp, L1_cond_btemp, L1_cond_Wout, L1_cond_gamma, L1_cond_beta)
    return x

_drawn_inputs = setup_inputs


def setup_inputs(seed=0):
    import zlib

    import numpy as np

    out = dict(_drawn_inputs(seed))
    spreads = {'condB_bn2': (0.0, 2.0),
     'L1_cond_bg': (-0.5, 0.6),
     'L1_cond_bn1': (0.0, 2.0),
     'L1_cond_bsoma': (0.0, 0.1),
     'L1_cond_btemp': (0.0, 0.508),
     'L1_cond_gamma': (1.0, 0.2),
     'L1_cond_beta': (0.0, 0.1)}
    factors = {'condB_tauraws': 8.0, 'cond_256': 8.0, 'cond_1024': 64.0, 'L1_cond_Wn1': 8.0}
    for name, (base, spread) in spreads.items():
        noise = np.random.default_rng([zlib.crc32(name.encode()), seed]).standard_normal(out[name].shape)
        drawn = base * np.exp(spread * noise) if base else spread * noise
        out[name] = jnp.asarray(drawn.astype(out[name].dtype))
    for name, factor in factors.items():
        out[name] = (out[name] * factor).astype(out[name].dtype)
    return out
```

```python
from contextlib import ExitStack

import concourse.bass as bass
from concourse import mybir

F32 = mybir.dt.float32
F32R = mybir.dt.float32r
I32 = mybir.dt.int32
ALU = mybir.AluOpType
ACT = mybir.ActivationFunctionType
AX_X = mybir.AxisListType.X

P = 128


def build(nc, x, f, stage, tau, wn2T, bn2, blendT, embed, tau_ctx, wgT, bg, wn1T, bn1, wsT, bs,
          wtT, bt, woT, gamma, beta, out):
    B, S, D = x.shape
    NB = 2
    PAIRS = B // NB
    ST = S // P
    CT = D // P
    NT = blendT.shape[1]
    NH = wn1T.shape[1]
    NSTAGE = embed.shape[0]
    CH = 16
    REP = P // NT
    KT = S // (REP * CH)
    N = NB * S
    CHN = N // CH
    EPS = 1e-5
    HC = CH // 2
    GROUPS = [(j,) for j in range(HC)] + [(j, j + 1) for j in range(HC, CH, 2)]
    NG = len(GROUPS)

    def width(j):
        return max((CH - j + 1) // 2 * 2, HC)

    NPROD = 4

    xv = x.rearrange("(q b) (t p) d -> q p b t d", b=NB, p=P)
    fv = f.rearrange("(q b) (t p) d -> q p b t d", b=NB, p=P)
    ov = out.rearrange("(q b) (t p) d -> q p b t d", b=NB, p=P)

    with ExitStack() as ctx:
        def sb(name, shape, dt=F32):
            return ctx.enter_context(nc.sbuf_tensor(name, shape, dt))

        def sem(name):
            return ctx.enter_context(nc.semaphore(name))

        ident = sb("ident", [P, P])
        zeros = sb("zeros", [P, S])
        WgT = sb("WgT", [P, 2 * CT, D])
        Wn1T = sb("Wn1T", [P, CT, P])
        Wn2T = sb("Wn2T", [P, REP, NT])
        WsT = sb("WsT", [P, CT, D])
        WtT = sb("WtT", [P, CT, D])
        WoT = sb("WoT", [P, CT, D])
        gammaB = sb("gammaB", [P, D])
        betaB = sb("betaB", [P, D])
        bgC = sb("bgC", [P, CT])
        bsC = sb("bsC", [P, CT])
        btC = sb("btC", [P, CT])
        bn1C = sb("bn1C", [P, 1])
        bn2C = sb("bn2C", [P, 1])
        tauC = sb("tauC", [P, 1])
        alphaC = sb("alphaC", [P, 1])
        tauX = sb("tauX", [P, 1])
        alphaX = sb("alphaX", [P, 1])
        decayX = sb("decayX", [P, S])
        blT = sb("blT", [P, CT, NT])
        blM = sb("blM", [P, CT])
        blS = sb("blS", [P, CT])
        blR = sb("blR", [P, CT])
        w4 = sb("w4", [P, CT, REP, NT])
        wrep = sb("wrep", [P, D])
        powers = sb("powers", [P, S + 1])
        chunkend = sb("chunkend", [P, P])
        leave = sb("leave", [P, P // CH, NT])
        read = sb("read", [P, KT, S])
        near = sb("near", [P, CH, D], F32R)
        stI = sb("stI", [NSTAGE, B], I32)
        stF = sb("stF", [NSTAGE, B])
        rowI = sb("rowI", [NSTAGE, 1], I32)
        rowF = sb("rowF", [NSTAGE, 1])
        hot = sb("hot", [NSTAGE, B])
        emb = sb("emb", [NSTAGE, S])
        biasT = sb("biasT", [P, ST, B])
        negHalf = sb("negHalf", [P, NB * ST])
        xn = sb("xn", [P, 2, NB, ST, D])
        kn = sb("kn", [P, 2, NB, ST, D])
        qn = sb("qn", [P, NB, ST, D])
        qT = sb("qT", [P, CT, NB, S])
        kT = sb("kT", [P, CT, NB, S])
        prob = sb("prob", [P, NB, ST, S])
        probT = sb("probT", [P, ST, NB, S])
        rowmax = sb("rowmax", [P, NB, ST])
        negmax = sb("negmax", [P, NB, ST])
        rowsum = sb("rowsum", [P, NB, ST])
        rowinv = sb("rowinv", [P, NB, ST])
        x2n = sb("x2n", [P, NB, ST, D])
        x2b = sb("x2b", [P, 2, NB, ST, D])
        x2T = sb("x2T", [P, CT, NB, S])
        cxT = sb("cxT", [P, CT, NB, S])
        h1 = sb("h1", [P, N])
        thM = sb("thM", [P, N])
        mN = sb("mN", [P, NB * ST, NT])
        ms = sb("ms", [P, N], F32R)
        thG = sb("thG", [P, CT, N])
        gT = sb("gT", [P, CT, N])
        gn = sb("gn", [P, NB, ST, D])
        lv = sb("lv", [P, NB * ST, P // CH, NT])
        Hw = sb("Hw", [P, NB, KT, D])
        prod = sb("prod", [P, NPROD, CT, N])
        acc = sb("acc", [P, 2, CT, N])
        soma = sb("soma", [P, 2, CT, N])
        thT = sb("thT", [P, CT, N])
        sgT = sb("sgT", [P, CT, N])
        stats = sb("stats", [P, NB * ST, 6])
        both = sb("both", [P, NB * ST, 2])
        dif = sb("dif", [P, NB * ST])
        dif2 = sb("dif2", [P, NB * ST])
        mean = sb("mean", [P, NB * ST])
        varE = sb("varE", [P, NB * ST])
        rstd = sb("rstd", [P, NB * ST])
        cen = sb("cen", [P, NB * ST, D])
        y = sb("y", [P, 2, NB, ST, D])
        wide = prod[:, :, :, :].rearrange("p i t n -> p (i t n)").rearrange("p (j d) -> p j d", d=D)
        assert NPROD * CT * N == CH * D and CH % NPROD == 0

        nearP = [ctx.enter_context(nc.psum_tensor(f"nearP{i}", [P, CT, N], F32)) for i in range(2)]
        work = [ctx.enter_context(nc.psum_tensor(f"work{i}", [P, 2, N], F32)) for i in range(2)]

        w_in = sem("w_in")
        x_in = [sem(f"x_in{i}") for i in range(2)]
        k_in = [sem(f"k_in{i}") for i in range(2)]
        y_out = [sem(f"y_out{i}") for i in range(2)]
        w_late = sem("w_late")
        c_zero = sem("c_zero")
        c_ident, c_row, c_mask = sem("c_ident"), sem("c_row"), sem("c_mask")
        c_exp, c_blexp = sem("c_exp"), sem("c_blexp")
        c_bias_ps, c_wrep_ps, c_leave_ps = sem("c_bias_ps"), sem("c_wrep_ps"), sem("c_leave_ps")
        c_hot, c_blmax, c_w4 = sem("c_hot"), sem("c_blmax"), sem("c_w4")
        c_chunkend, c_leave, c_const = sem("c_chunkend"), sem("c_leave"), sem("c_const")
        c_dve = sem("c_dve")
        q_added = sem("q_added")
        qT_ps, qT_sb = sem("qT_ps"), sem("qT_sb")
        kT_ps, kT_sb = sem("kT_ps"), sem("kT_sb")
        score_ps = sem("score_ps")
        max_dv, negmax_dv = sem("max_dv"), sem("negmax_dv")
        prob_sb = sem("prob_sb")
        rowinv_dv = sem("rowinv_dv")
        pT_ps, pT_sb = sem("pT_ps"), sem("pT_sb")
        att_ps = sem("att_ps")
        x2_dv = sem("x2_dv")
        x2b_pool = sem("x2b_pool")
        x2T_ps, x2T_sb = sem("x2T_ps"), sem("x2T_sb")
        cx_dv = sem("cx_dv")
        h1_ps, h1_sb = sem("h1_ps"), sem("h1_sb")
        g_ps, thG_sb, g_dv = sem("g_ps"), sem("thG_sb"), sem("g_dv")
        m_ps, thM_sb, ms_dv = sem("m_ps"), sem("thM_sb"), sem("ms_dv")
        mN_ps, mN_sb = sem("mN_ps"), sem("mN_sb")
        lv_pool = sem("lv_pool")
        gn_ps, gn_sb = sem("gn_ps"), sem("gn_sb")
        st_ps, Hw_dv = sem("st_ps"), sem("Hw_dv")
        far_ps, far_sb = sem("far_ps"), sem("far_sb")
        near_ps, near_dv, near_pool = sem("near_ps"), sem("near_dv"), sem("near_pool")
        soma_ps, soma_sb = sem("soma_ps"), sem("soma_sb")
        tg_ps, tg_sb, sg_dv = sem("tg_ps"), sem("tg_sb"), sem("sg_dv")
        o_ps = sem("o_ps")
        st_dv, both_dv, mean_dv, var_dv = sem("st_dv"), sem("both_dv"), sem("mean_dv"), sem("var_dv")
        rstd_pool = sem("rstd_pool")
        cen_dv, y_dv = sem("cen_dv"), sem("y_dv")

        NLOAD = 13 + 2 * REP
        NLATE = 2 + REP
        NZERO = 7

        def need(eng, s, value):
            if not isinstance(value, int) or value > 0:
                eng.wait_ge(s, value)

        def steps(eng, body):
            body(-1, True, False, False, 0, 0)
            body(0, True, True, False, 1, 0)
            body(1, True, True, True, 0, 1)
            body(2, True, True, True, 1, 1)
            with eng.Fori(0, (PAIRS - 4) // 2) as i:
                body(i * 2 + 3, True, True, True, 0, i + 2)
                body(i * 2 + 4, True, True, True, 1, i + 2)
            body(PAIRS - 1, False, True, True, 0, PAIRS // 2)
            body(PAIRS, False, False, True, 1, PAIRS // 2)

        block = ctx.enter_context(nc.Block())

        @block.sync
        def _(sp):
            def load(pair, par):
                sp.dma_start(xn[:, par], xv[pair]).then_inc(x_in[par], 16)
                sp.dma_start(kn[:, par], fv[pair]).then_inc(k_in[par], 16)

            load(0, 0)
            loads = [
                (stI[:, :], stage.partition_broadcast(NSTAGE)), (emb[:, :], embed),
                (tauX[:, :], tau_ctx.partition_broadcast(P)),
                (blT[:, :, :], blendT.rearrange("(t p) n -> p t n", p=P)),
                (WgT[:, :, :], wgT.rearrange("(t p) n -> p t n", p=P)),
                (WsT[:, :, :], wsT.rearrange("(t p) n -> p t n", p=P)),
                (WtT[:, :, :], wtT.rearrange("(t p) n -> p t n", p=P)),
                (WoT[:, :, :], woT.rearrange("(t p) n -> p t n", p=P)),
                (gammaB[:, :], gamma.partition_broadcast(P)), (betaB[:, :], beta.partition_broadcast(P)),
                (bgC[:, :], bg), (bsC[:, :], bs), (btC[:, :], bt),
            ]
            for dst, src in loads:
                sp.dma_start(dst, src).then_inc(w_in, 16)
            for r in range(REP):
                sp.dma_start(tauC[r * NT:(r + 1) * NT, :], tau.rearrange("(n o) -> n o", o=1)).then_inc(w_in, 16)
                sp.dma_start(bn2C[r * NT:(r + 1) * NT, :], bn2.rearrange("(n o) -> n o", o=1)).then_inc(w_in, 16)
            assert len(loads) + 2 * REP == NLOAD
            sp.wait_ge(c_zero, NZERO)
            sp.dma_start(Wn1T[:, :, 0:NH], wn1T.rearrange("(t p) n -> p t n", p=P)).then_inc(w_late, 16)
            sp.dma_start(bn1C[0:NH, :], bn1.rearrange("(n o) -> n o", o=1)).then_inc(w_late, 16)
            for r in range(REP):
                sp.dma_start(Wn2T[0:NH, r, :], wn2T).then_inc(w_late, 16)
            load(1, 1)

            def load_next(s, par):
                need(sp, x2_dv, (s + 1) * 4)
                load(s + 2, par)

            def store_last(s, par):
                need(sp, y_dv, s * 4)
                sp.dma_start(ov[s - 1], y[:, par]).then_inc(y_out[par], 16)

            load_next(0, 0)
            with sp.Fori(0, (PAIRS - 4) // 2) as i:
                for u in range(2):
                    load_next(i * 2 + 1 + u, 1 - u)
                    store_last(i * 2 + 1 + u, u)
            load_next(PAIRS - 3, 1)
            for s in range(PAIRS - 3, PAIRS + 1):
                store_last(s, (s + 1) % 2)
            for par in range(2):
                sp.wait_ge(y_out[par], 16 * (PAIRS // 2))

        @block.gpsimd
        def _(pool):
            pool.memset(ident[:, :], 0.0).then_inc(c_zero, 1)
            pool.memset(zeros[:, :], 0.0).then_inc(c_zero, 1)
            pool.memset(Wn1T[:, :, :], 0.0).then_inc(c_zero, 1)
            pool.memset(Wn2T[:, :, :], 0.0).then_inc(c_zero, 1)
            pool.memset(bn1C[:, :], 0.0).then_inc(c_zero, 1)
            pool.memset(read[:, :, :], 0.0).then_inc(c_zero, 1)
            pool.memset(negHalf[:, :], -0.5).then_inc(c_zero, 1)
            pool.wait_ge(c_zero, NZERO)
            pool.affine_select(out=ident[:, :], in_=ident[:, :], compare_op=ALU.not_equal, fill=1.0, base=0,
                               pattern=[[-1, P]], channel_multiplier=1).then_inc(c_ident, 1)
            pool.iota(rowI[:, :], pattern=[[0, 1]], base=0, channel_multiplier=1).then_inc(c_row, 1)
            pool.wait_ge(c_leave, 1)
            pool.affine_select(out=leave[:, :, :], in_=leave[:, :, :], compare_op=ALU.is_ge, fill=0.0, base=0,
                               pattern=[[-CH, P // CH], [0, NT]], channel_multiplier=1).then_inc(c_mask, 1)
            pool.wait_ge(c_mask, 1)
            pool.affine_select(out=leave[:, :, :], in_=leave[:, :, :], compare_op=ALU.is_ge, fill=0.0,
                               base=CH - 1, pattern=[[CH, P // CH], [0, NT]],
                               channel_multiplier=-1).then_inc(c_mask, 1)
            pool.wait_ge(c_mask, 2)
            pool.wait_ge(w_in, 16 * NLOAD)

            def body(s, a, r, z, pa, h):
                pr = 1 - pa
                if r:
                    for j in range(CH):
                        if j == 0:
                            pool.wait_ge(far_sb, (s + 1) * 2)
                        need(pool, near_dv, s * CH + j + 1)
                        if j:
                            need(pool, near_pool, s * CH + j)
                        d = acc[:, pr].rearrange("p t (c k) -> p t c k", k=CH)[:, :, :, j:CH]
                        n = CH - j
                        src = prod[:, j % NPROD, :, 0:CHN * n].rearrange("p t (c k) -> p t c k", k=n)
                        pool.tensor_tensor(d, d, src, ALU.add).then_inc(near_pool, 1)
                        if j == CH // 2 and z:
                            tail(s)
                elif z:
                    tail(s)
                if a:
                    need(pool, x2_dv, (s + 2) * 4)
                    if z:
                        need(pool, y_dv, s * 4)
                    bb = betaB[:, :].unsqueeze(1).to_broadcast([P, NB * ST, D])
                    pool.tensor_tensor(x2b[:, pa].rearrange("p b t d -> p (b t) d"),
                                       x2n[:, :, :, :].rearrange("p b t d -> p (b t) d"), bb,
                                       ALU.add).then_inc(x2b_pool, 1)
                    need(pool, mN_sb, s + 2)
                    if r:
                        need(pool, st_ps, (s + 1) * 4)
                    each = [P, NB * ST, P // CH, NT]
                    pool.tensor_tensor(lv[:, :, :, :], mN[:, :, :].unsqueeze(2).to_broadcast(each),
                                       leave[:, :, :].unsqueeze(1).to_broadcast(each),
                                       ALU.mult).then_inc(lv_pool, 1)

            def tail(s):
                need(pool, var_dv, s)
                pool.tensor_tensor(rstd[:, :], varE[:, :], negHalf[:, :], ALU.pow).then_inc(rstd_pool, 1)

            steps(pool, body)

        @block.scalar
        def _(act):
            act.wait_ge(w_in, 16 * NLOAD)
            act.activation(alphaC[:, :], tauC[:, :], ACT.Exp).then_inc(c_exp, 1)
            act.activation(alphaX[:, :], tauX[:, :], ACT.Exp).then_inc(c_exp, 1)
            act.wait_ge(c_blmax, 1)
            for t in range(CT):
                act.activation(blT[:, t, :], blT[:, t, :], ACT.Exp, bias=blM[:, t:t + 1],
                               accum_out=blS[:, t:t + 1]).then_inc(c_blexp, 1)
            act.wait_ge(c_const, 1)

            def body(s, a, r, z, pa, h):
                pr = 1 - pa
                if a:
                    for t in range(CT):
                        need(act, qT_ps, (s + 1) * 2 + t + 1)
                        act.copy(qT[:, t].rearrange("p b s -> p (b s)"), work[0][:, t, :]).then_inc(qT_sb, 1)
                    for t in range(CT):
                        need(act, kT_ps, (s + 1) * 2 + t + 1)
                        act.copy(kT[:, t].rearrange("p b s -> p (b s)"), work[1][:, t, :]).then_inc(kT_sb, 1)
                if r:
                    for t in range(CT):
                        need(act, far_ps, s * 2 + t + 1)
                        if z and t == 0:
                            need(act, tg_ps, (s - 1) * 2)
                        act.copy(acc[:, pr, t, :], work[0][:, t, :]).then_inc(far_sb, 1)
                if a:
                    for b in range(NB):
                        need(act, negmax_dv, (s + 1) * 2 + b + 1)
                        if b == 0 and r:
                            need(act, pT_ps, (s + 1) * 2)
                            need(act, rowinv_dv, s + 1)
                        for t in range(ST):
                            act.activation(prob[:, b, t, :], work[1][:, b, t * S:(t + 1) * S], ACT.Exp,
                                           bias=negmax[:, b, t:t + 1],
                                           accum_out=rowsum[:, b, t:t + 1]).then_inc(prob_sb, 1)
                if z:
                    need(act, sg_dv, (s - 1) * 2)
                    for t in range(CT):
                        need(act, tg_ps, (s - 1) * 2 + t + 1)
                        act.activation(thT[:, t, :], work[0][:, t, :], ACT.Tanh, bias=btC[:, t:t + 1],
                                       scale=0.5).then_inc(tg_sb, 1)
                if a:
                    for t in range(ST):
                        need(act, pT_ps, (s + 1) * 2 + t + 1)
                        act.copy(probT[:, t].rearrange("p b s -> p (b s)"), work[1][:, t, :]).then_inc(pT_sb, 1)
                if r:
                    for t in range(CT):
                        need(act, soma_ps, s * 2 + t + 1)
                        act.activation(soma[:, pr, t, :], work[0][:, t, :], ACT.Gelu,
                                       bias=bsC[:, t:t + 1]).then_inc(soma_sb, 1)
                if a:
                    for t in range(CT):
                        need(act, x2T_ps, (s + 1) * 2 + t + 1)
                        act.copy(x2T[:, t].rearrange("p b s -> p (b s)"), work[1][:, t, :]).then_inc(x2T_sb, 1)
                    need(act, h1_ps, s + 2)
                    act.activation(h1[:, :], work[0][:, 0, :], ACT.Gelu, bias=bn1C[:, 0:1]).then_inc(h1_sb, 1)
                    for t in range(CT):
                        need(act, g_ps, (s + 1) * 2 + t + 1)
                        act.activation(thG[:, t, :], work[1][:, t, :], ACT.Tanh, bias=bgC[:, t:t + 1],
                                       scale=0.5).then_inc(thG_sb, 1)
                    need(act, m_ps, s + 2)
                    act.activation(thM[:, :], work[0][:, 0, :], ACT.Tanh, bias=bn2C[:, 0:1],
                                   scale=0.5).then_inc(thM_sb, 1)
                    need(act, mN_ps, s + 2)
                    if r:
                        need(act, lv_pool, s + 1)
                    act.activation(mN[:, :, :], work[0][:, 1, :].rearrange("p (q n) -> p q n", n=P)[:, :, 0:NT],
                                   ACT.Copy, bias=2.0).then_inc(mN_sb, 1)
                    for b in range(NB):
                        need(act, gn_ps, (s + 1) * 2 + b + 1)
                        act.copy(gn[:, b].rearrange("p t d -> p (t d)"), work[1][:, b, :]).then_inc(gn_sb, 1)

            steps(act, body)

        @block.tensor
        def _(pe):
            pe.wait_ge(c_ident, 1)
            pe.wait_ge(c_hot, 1)
            for t in range(ST):
                ins = pe.matmul(work[0][:, 0, t * B:(t + 1) * B], emb[:, t * P:(t + 1) * P], hot[:, :],
                                start=True, stop=True)
            ins.then_inc(c_bias_ps, 1)
            pe.wait_ge(c_w4, 1)
            for t in range(CT):
                ins = pe.transpose(work[1][:, 0, t * P:(t + 1) * P],
                                   w4[:, t].rearrange("p r n -> p (r n)"), ident[:, :])
            ins.then_inc(c_wrep_ps, 1)
            pe.wait_ge(c_chunkend, 1)
            pe.transpose(work[1][:, 1, 0:P], chunkend[:, :], ident[:, :]).then_inc(c_leave_ps, 1)
            pe.wait_ge(c_const, 1)

            def transposes(dst, src_of, done):
                for t in range(2):
                    for i in range(N // P):
                        ins = pe.transpose(dst[:, t, i * P:(i + 1) * P], src_of(t, i), ident[:, :])
                    ins.then_inc(done, 1)

            def project(dst, weights, parts, done):
                for e in range(CT):
                    for k, part in enumerate(parts):
                        ins = pe.matmul(dst[:, e, :], weights[:, k, e * P:(e + 1) * P], part,
                                        start=(k == 0), stop=(k == len(parts) - 1))
                    ins.then_inc(done, 1)

            def body(s, a, r, z, pa, h):
                pr = 1 - pa

                def near_group(g):
                    if not r:
                        return
                    p = nearP[g % 2]
                    if g == 0:
                        need(pe, ms_dv, (s + 1) * 2)
                    last = GROUPS[g - 2][-1] + 1 if g >= 2 else GROUPS[NG - 2 + g][-1] + 1 - CH
                    need(pe, near_dv, s * CH + last)
                    for t in range(CT):
                        at = 0
                        for j in GROUPS[g]:
                            n = width(j)
                            ins = pe.matmul(p[:, t, at:at + CHN * n], near[:, j, t * P:(t + 1) * P],
                                            ms[:, :].rearrange("p (c k) -> p c k", k=CH)[:, :, 0:n],
                                            start=True, stop=True)
                            at += CHN * n
                    ins.then_inc(near_ps, 1)

                def states(b, dst):
                    for m in range(KT):
                        st = m // (KT // ST)
                        off = (m % (KT // ST)) * REP
                        ins = pe.matmul(dst[:, m // 2, (m % 2) * D:(m % 2 + 1) * D],
                                        lv[:, b * ST + st, off:off + REP, :].rearrange("p c n -> p (c n)"),
                                        gn[:, b, st, :], start=True, stop=True)
                        if m % 2:
                            ins.then_inc(st_ps, 1)

                if a:
                    need(pe, q_added, s + 2)
                    if r:
                        need(pe, mN_sb, s + 1)
                    transposes(work[0], lambda t, i: qn[:, i // ST, i % ST, t * P:(t + 1) * P], qT_ps)
                if r:
                    need(pe, gn_sb, (s + 1) * 2)
                    need(pe, lv_pool, s + 1)
                    states(0, work[1])
                    if a:
                        need(pe, qT_sb, (s + 2) * 2)
                    states(1, work[0])
                    near_group(0)
                if a:
                    pe.wait_ge(k_in[pa], (h + 1) * 16)
                    if r:
                        need(pe, Hw_dv, s * 4 + 2)
                    transposes(work[1], lambda t, i: kn[:, pa, i // ST, i % ST, t * P:(t + 1) * P], kT_ps)
                near_group(1)
                if r:
                    need(pe, Hw_dv, (s + 1) * 4)
                    for t in range(CT):
                        for b in range(NB):
                            for m in range(KT):
                                ins = pe.matmul(work[0][:, t, b * S:(b + 1) * S],
                                                Hw[:, b, m, t * P:(t + 1) * P], read[:, m, :],
                                                start=(m == 0), stop=(m == KT - 1))
                        ins.then_inc(far_ps, 1)
                near_group(2)
                if a:
                    need(pe, qT_sb, (s + 2) * 2)
                    need(pe, kT_sb, (s + 2) * 2)
                    for b in range(NB):
                        for t in range(ST):
                            for k in range(CT):
                                ins = pe.matmul(work[1][:, b, t * S:(t + 1) * S],
                                                qT[:, k, b, t * P:(t + 1) * P], kT[:, k, b, :],
                                                start=(k == 0), stop=(k == CT - 1))
                        ins.then_inc(score_ps, 1)
                near_group(3)
                if z:
                    need(pe, near_pool, s * CH)
                    if r:
                        need(pe, far_sb, (s + 1) * 2)
                    else:
                        need(pe, cen_dv, (s - 1) * 4)
                    project(work[0], WtT, [acc[:, pa, k, :] for k in range(CT)], tg_ps)
                near_group(4)
                if a:
                    need(pe, prob_sb, (s + 2) * 4)
                    transposes(work[1], lambda t, i: prob[:, i // ST, i % ST, t * P:(t + 1) * P], pT_ps)
                near_group(5)
                if r:
                    if z:
                        need(pe, tg_sb, s * 2)
                    elif a:
                        need(pe, far_sb, (s + 1) * 2)
                    project(work[0], WsT, [x2T[:, k].rearrange("p b s -> p (b s)") for k in range(CT)], soma_ps)
                near_group(6)
                if a:
                    need(pe, pT_sb, (s + 2) * 2)
                    for b in range(NB):
                        for t in range(ST):
                            for k in range(ST):
                                ins = pe.matmul(work[1][:, b, t * D:(t + 1) * D],
                                                probT[:, k, b, t * P:(t + 1) * P], kn[:, pa, b, k, :],
                                                start=(k == 0), stop=(k == ST - 1))
                        ins.then_inc(att_ps, 1)
                near_group(7)
                if z:
                    need(pe, sg_dv, s * 2)
                    if r:
                        need(pe, soma_sb, (s + 1) * 2)
                    for b in range(NB):
                        for t in range(ST):
                            for k in range(CT):
                                ins = pe.matmul(work[0][:, b, t * D:(t + 1) * D],
                                                sgT[:, k, b * S + t * P:b * S + (t + 1) * P], WoT[:, k, :],
                                                start=(k == 0), stop=(k == CT - 1))
                        ins.then_inc(o_ps, 1)
                near_group(8)
                if a:
                    need(pe, x2_dv, (s + 2) * 4)
                    transposes(work[1], lambda t, i: x2n[:, i // ST, i % ST, t * P:(t + 1) * P], x2T_ps)
                near_group(9)
                near_group(10)
                if a:
                    need(pe, x2T_sb, (s + 2) * 2)
                    if z:
                        need(pe, cen_dv, s * 4)
                    elif r:
                        need(pe, soma_sb, (s + 1) * 2)
                    for k in range(CT):
                        ins = pe.matmul(work[0][:, 0, :], Wn1T[:, k, :], x2T[:, k].rearrange("p b s -> p (b s)"),
                                        start=(k == 0), stop=(k == CT - 1))
                    ins.then_inc(h1_ps, 1)
                    parts = [v[:, k].rearrange("p b s -> p (b s)") for v in (x2T, cxT) for k in range(CT)]
                    for e in range(CT):
                        for k, part in enumerate(parts):
                            if e == 0 and k == CT:
                                need(pe, cx_dv, (s + 2) * 4)
                            ins = pe.matmul(work[1][:, e, :], WgT[:, k, e * P:(e + 1) * P], part,
                                            start=(k == 0), stop=(k == len(parts) - 1))
                        ins.then_inc(g_ps, 1)
                    need(pe, h1_sb, s + 2)
                    pe.matmul(work[0][:, 0, :], Wn2T[:, :, :].rearrange("p r n -> p (r n)"), h1[:, :],
                              start=True, stop=True).then_inc(m_ps, 1)
                near_group(11)
                if a:
                    need(pe, thM_sb, s + 2)
                    for i in range(N // P):
                        ins = pe.transpose(work[0][:, 1, i * P:(i + 1) * P], thM[:, i * P:(i + 1) * P],
                                           ident[:, :])
                    ins.then_inc(mN_ps, 1)
                    need(pe, g_dv, (s + 2) * 2)
                    for b in range(NB):
                        for t in range(ST):
                            for k in range(CT):
                                ins = pe.transpose(work[1][:, b, t * D + k * P:t * D + (k + 1) * P],
                                                   gT[:, k, b * S + t * P:b * S + (t + 1) * P], ident[:, :])
                        ins.then_inc(gn_ps, 1)

            steps(pe, body)

        @block.vector
        def _(dve):
            chain = [0]

            def link(ins):
                chain[0] += 1
                ins.then_inc(c_dve, 1)
                dve.wait_ge(c_dve, chain[0])

            dve.wait_ge(w_in, 16 * NLOAD)
            dve.wait_ge(c_row, 1)
            link(dve.tensor_copy(stF[:, :], stI[:, :]))
            link(dve.tensor_copy(rowF[:, :], rowI[:, :]))
            dve.tensor_scalar(hot[:, :], stF[:, :], rowF[:, 0:1], None, ALU.is_equal).then_inc(c_hot, 1)
            link(dve.tensor_reduce(blM[:, :], blT[:, :, :], AX_X, ALU.max))
            dve.tensor_scalar(blM[:, :], blM[:, :], -1.0, None, ALU.mult).then_inc(c_blmax, 1)
            dve.wait_ge(c_exp, 2)
            for a_ in (alphaC, alphaX):
                link(dve.tensor_scalar(a_[:, :], a_[:, :], 1.0, None, ALU.add))
                link(dve.reciprocal(a_[:, :], a_[:, :]))
            dve.wait_ge(c_zero, NZERO)
            dve.tensor_scalar(decayX[:, :], zeros[:, :], alphaX[:, 0:1], None, ALU.add)
            dve.memset(powers[:, 0:1], 1.0)
            link(dve.tensor_tensor_scan(powers[:, 1:S + 1], alphaC[:, 0:1].to_broadcast([P, S]), zeros[:, :],
                                        1.0, ALU.mult, ALU.add))
            ce = chunkend[:, :].rearrange("p (c k) -> p c k", k=CH)
            for k in range(CH):
                ins = dve.tensor_copy(ce[:, :, k], powers[:, CH - 1 - k:CH - k].to_broadcast([P, P // CH]))
            ins.then_inc(c_chunkend, 1)
            dve.wait_ge(c_blexp, CT)
            link(dve.reciprocal(blR[:, :], blS[:, :]))
            for t in range(CT):
                for r in range(REP):
                    ins = dve.tensor_scalar(w4[:, t, r, :], blT[:, t, :], blR[:, t:t + 1], 0.25,
                                            ALU.mult, ALU.mult)
            ins.then_inc(c_w4, 1)
            for c in range(S // CH - 1):
                kk, m, t0 = c % REP, c // REP, (c + 1) * CH
                dve.tensor_copy(read[kk * NT:(kk + 1) * NT, m, t0:S], powers[kk * NT:(kk + 1) * NT, 1:1 + S - t0])
            dve.wait_ge(c_bias_ps, 1)
            dve.tensor_copy(biasT[:, :, :].rearrange("p t b -> p (t b)"), work[0][:, 0, 0:ST * B])
            dve.wait_ge(c_wrep_ps, 1)
            link(dve.tensor_copy(wrep[:, :], work[1][:, 0, 0:D]))
            dve.wait_ge(c_leave_ps, 1)
            dve.tensor_copy(leave[:, :, :],
                            work[1][:, 1, 0:NT].unsqueeze(1).to_broadcast([P, P // CH, NT])).then_inc(c_leave, 1)
            for j in range(CH):
                ins = dve.tensor_scalar(wide[:, j, :], wrep[:, :], powers[:, j:j + 1], None, ALU.mult)
            link(ins)
            link(dve.tensor_copy(near[:, :, :], wide))
            for r in range(1, REP, 2):
                rows = slice(r * NT, (r + 1) * NT)
                dve.tensor_tensor(near[rows], wide[rows], near[rows].bitcast(F32), ALU.subtract)
            for v in (bgC, btC, bn2C):
                dve.tensor_scalar(v[:, :], v[:, :], 0.5, None, ALU.mult)
            link(dve.tensor_scalar(WoT[:, :, :], WoT[:, :, :], 0.5, None, ALU.mult))
            dve.wait_ge(w_late, 16 * NLATE)
            link(dve.memset(rowmax[:, :, :], 0.0))
            dve.memset(rowinv[:, :, :], 0.0).then_inc(c_const, 1)

            def body(s, a, r, z, pa, h):
                def near_group(g):
                    if not r:
                        return
                    need(dve, near_ps, s * NG + g + 1)
                    at = 0
                    for j in GROUPS[g]:
                        n, m = width(j), CH - j
                        src = nearP[g % 2][:, :, at:at + CHN * n].rearrange("p t (c k) -> p t c k", k=n)
                        gv = gT[:, :, :].rearrange("p t (c k) -> p t c k", k=CH)
                        dst = prod[:, j % NPROD, :, 0:CHN * m].rearrange("p t (c k) -> p t c k", k=m)
                        need(dve, near_pool, s * CH + j + 1 - NPROD)
                        dve.tensor_tensor(dst, src[:, :, :, 0:m], gv[:, :, :, 0:m], ALU.mult)\
                           .then_inc(near_dv, 1)
                        at += CHN * n

                if a:
                    dve.wait_ge(x_in[pa], (h + 1) * 16)
                    need(dve, qT_ps, (s + 1) * 2)
                    for b in range(NB):
                        for t in range(ST):
                            at = (s + 1) * NB + b
                            ins = dve.tensor_scalar(qn[:, b, t, :], xn[:, pa, b, t, :],
                                                    biasT[:, t, bass.ds(at, 1)], None, ALU.add)
                    ins.then_inc(q_added, 1)
                if r:
                    for b in range(NB):
                        for k in range(2):
                            need(dve, st_ps, s * 4 + 2 * b + k + 1)
                            dve.tensor_tensor(
                                Hw[:, b, 2 * k:2 * k + 2, :],
                                work[1 - b][:, k, :].rearrange("p (m d) -> p m d", d=D),
                                wrep[:, :].unsqueeze(1).to_broadcast([P, 2, D]), ALU.mult).then_inc(Hw_dv, 1)
                near_group(0)
                near_group(1)
                if a:
                    for b in range(NB):
                        need(dve, score_ps, (s + 1) * 2 + b + 1)
                        dve.tensor_reduce(rowmax[:, b, :], work[1][:, b, :].rearrange("p (t s) -> p t s", s=S),
                                          AX_X, ALU.max).then_inc(max_dv, 1)
                        need(dve, max_dv, (s + 1) * 2 + b + 1)
                        dve.tensor_scalar(negmax[:, b, :], rowmax[:, b, :], -1.0, None, ALU.mult)\
                           .then_inc(negmax_dv, 1)
                near_group(2)
                near_group(3)
                if z:
                    for t in range(CT):
                        need(dve, tg_sb, (s - 1) * 2 + t + 1)
                        dve.scalar_tensor_tensor(out=sgT[:, t, :], in0=thT[:, t, :], scalar=1.0,
                                                 in1=soma[:, pa, t, :], op0=ALU.add, op1=ALU.mult)\
                           .then_inc(sg_dv, 1)
                near_group(4)
                if a:
                    need(dve, prob_sb, (s + 2) * 4)
                    dve.reciprocal(rowinv[:, :, :], rowsum[:, :, :]).then_inc(rowinv_dv, 1)
                near_group(5)
                near_group(6)
                if a:
                    need(dve, rowinv_dv, s + 2)
                    if r:
                        need(dve, x2b_pool, s + 1)
                    for b in range(NB):
                        need(dve, att_ps, (s + 1) * 2 + b + 1)
                        for t in range(ST):
                            dve.scalar_tensor_tensor(
                                out=x2n[:, b, t, :], in0=work[1][:, b, t * D:(t + 1) * D],
                                scalar=rowinv[:, b, t:t + 1], in1=xn[:, pa, b, t, :],
                                op0=ALU.mult, op1=ALU.add).then_inc(x2_dv, 1)
                near_group(7)
                if z:
                    for q in range(NB * ST):
                        b, t = q // ST, q % ST
                        if t == 0:
                            need(dve, o_ps, (s - 1) * 2 + b + 1)
                        dve.bn_stats(stats[:, q, :], work[0][:, b, t * D:(t + 1) * D]).then_inc(st_dv, 1)
                    need(dve, st_dv, s * 4)
                    dve.tensor_tensor(both[:, :, :], stats[:, :, 1:3], stats[:, :, 4:6], ALU.add)\
                       .then_inc(both_dv, 1)
                    dve.tensor_tensor(dif[:, :], stats[:, :, 1], stats[:, :, 4], ALU.subtract)\
                       .then_inc(both_dv, 1)
                    need(dve, both_dv, s * 2)
                    dve.tensor_scalar(mean[:, :], both[:, :, 0], 0.5, None, ALU.mult).then_inc(mean_dv, 1)
                    dve.tensor_tensor(dif2[:, :], dif[:, :], dif[:, :], ALU.mult).then_inc(mean_dv, 1)
                    dve.tensor_scalar(varE[:, :], both[:, :, 1], 1.0 / D, EPS, ALU.mult, ALU.add)\
                       .then_inc(mean_dv, 1)
                    need(dve, mean_dv, s * 3)
                    dve.scalar_tensor_tensor(out=varE[:, :], in0=dif2[:, :], scalar=0.25, in1=varE[:, :],
                                             op0=ALU.mult, op1=ALU.add).then_inc(var_dv, 1)
                    for q in range(NB * ST):
                        b, t = q // ST, q % ST
                        dve.scalar_tensor_tensor(
                            out=cen[:, q, :], in0=work[0][:, b, t * D:(t + 1) * D], scalar=mean[:, q:q + 1],
                            in1=gammaB[:, :], op0=ALU.subtract, op1=ALU.mult).then_inc(cen_dv, 1)
                near_group(8)
                near_group(9)
                if a:
                    for k in range(CT):
                        need(dve, x2T_sb, (s + 1) * 2 + k + 1)
                        for b in range(NB):
                            dve.tensor_tensor_scan(cxT[:, k, b, :], decayX[:, :], x2T[:, k, b, :], 0.0,
                                                   ALU.mult, ALU.add).then_inc(cx_dv, 1)
                near_group(10)
                if z:
                    need(dve, rstd_pool, s)
                    need(dve, x2b_pool, s)
                    need(dve, cen_dv, s * 4)
                    need(dve, y_out[pa], (h - 1) * 16)
                    for q in range(NB * ST):
                        dve.scalar_tensor_tensor(
                            out=y[:, pa, q // ST, q % ST, :], in0=cen[:, q, :], scalar=rstd[:, q:q + 1],
                            in1=x2b[:, pa, q // ST, q % ST, :], op0=ALU.mult, op1=ALU.add).then_inc(y_dv, 1)
                near_group(11)
                if a:
                    need(dve, thM_sb, s + 2)
                    dve.tensor_scalar(ms[:, :], thM[:, :], 2.0, None, ALU.add).then_inc(ms_dv, 1)
                    need(dve, ms_dv, (s + 1) * 2 + 1)
                    up = slice(P // 2, P)
                    dve.scalar_tensor_tensor(out=ms[up, :], in0=thM[up, :], scalar=2.0,
                                             in1=ms[up, :].bitcast(F32), op0=ALU.add, op1=ALU.subtract)\
                       .then_inc(ms_dv, 1)
                    for t in range(CT):
                        need(dve, thG_sb, (s + 1) * 2 + t + 1)
                        dve.scalar_tensor_tensor(out=gT[:, t, :], in0=thG[:, t, :], scalar=1.0,
                                                 in1=x2T[:, t].rearrange("p b s -> p (b s)"),
                                                 op0=ALU.add, op1=ALU.mult).then_inc(g_dv, 1)

            steps(dve, body)


_OUT = (32, 256, 256)


def kernel(x, fside_BxSxS_0, itok_B_0_5, condB_tauraws, cond_256, condB_bn2, cond_1024, L0_cond_braak_embed,
           L1_cond_tau_ctx, L1_cond_Wg, L1_cond_bg, L1_cond_Wn1, L1_cond_bn1, L1_cond_Wsoma, L1_cond_bsoma,
           L1_cond_Wtemp, L1_cond_btemp, L1_cond_Wout, L1_cond_gamma, L1_cond_beta):
    import numpy as np
    import concourse.bacc as bacc
    from concourse.bass_utils import run_bass_kernel_spmd

    def by_partition(v):
        return np.asarray(v).reshape(-1, P).T

    arrays = {
        "x": x, "f": fside_BxSxS_0, "stage": itok_B_0_5, "tau": condB_tauraws,
        "wn2T": np.asarray(cond_256).T, "bn2": condB_bn2, "blendT": np.asarray(cond_1024).T,
        "embed": L0_cond_braak_embed, "tau_ctx": np.asarray(L1_cond_tau_ctx).reshape(1),
        "wgT": np.asarray(L1_cond_Wg).T, "bg": by_partition(L1_cond_bg), "wn1T": np.asarray(L1_cond_Wn1).T,
        "bn1": L1_cond_bn1, "wsT": np.asarray(L1_cond_Wsoma).T, "bs": by_partition(L1_cond_bsoma),
        "wtT": np.asarray(L1_cond_Wtemp).T, "bt": by_partition(L1_cond_btemp), "woT": np.asarray(L1_cond_Wout).T,
        "gamma": L1_cond_gamma, "beta": L1_cond_beta,
    }
    arrays = {"in_" + k: np.ascontiguousarray(v) for k, v in arrays.items()}
    nc = bacc.Bacc("TRN2", target_bir_lowering=False, num_devices=1)
    args = [nc.dram_tensor(k, v.shape, mybir.dt.from_np(v.dtype), kind="ExternalInput").ap()
            for k, v in arrays.items()]
    out = nc.dram_tensor("out", _OUT, F32, kind="ExternalOutput").ap()
    build(nc, *args, out)
    return run_bass_kernel_spmd(nc, [arrays], core_ids=[0]).results[0]["out"]
```

```python
from contextlib import ExitStack

import concourse.bass as bass
from concourse import mybir

F32 = mybir.dt.float32
F32R = mybir.dt.float32r
I32 = mybir.dt.int32
ALU = mybir.AluOpType
ACT = mybir.ActivationFunctionType
AX_X = mybir.AxisListType.X

P = 128


def build(nc, x_pos, f_pos, x_chn, f_chn, stage, tau, wn2T, bn2, blendT, embed, tau_ctx, wgT, bg, wn1T, bn1, wsT, bs,
          wtT, bt, woT, gamma, beta, out):
    PAIRS, _, NB, ST, D = x_pos.shape
    _, _, CT, _, S = x_chn.shape
    B = PAIRS * NB
    NT = blendT.shape[1]
    NH = wn1T.shape[1]
    NSTAGE = embed.shape[0]
    CH = 16
    REP = P // NT
    KT = S // (REP * CH)
    N = NB * S
    CHN = N // CH
    CS = S // CH
    SLOT = [t * CS - t * (t - 1) // 2 * (P // CH) for t in range(ST + 1)]
    EPS = 1e-5
    HC = CH // 2
    GROUPS = [(j,) for j in range(HC)] + [(j, j + 1) for j in range(HC, CH, 2)]
    NG = len(GROUPS)

    def width(j):
        return max((CH - j + 1) // 2 * 2, HC)

    NPROD = 4
    NADD = CH - 1
    FAR_AFTER = 9

    bias_d = nc.dram_tensor("bias_rows", (PAIRS, NB, S), F32, kind="Internal").ap()

    with ExitStack() as ctx:
        def sb(name, shape, dt=F32):
            return ctx.enter_context(nc.sbuf_tensor(name, shape, dt))

        def sem(name):
            return ctx.enter_context(nc.semaphore(name))

        ident = sb("ident", [P, P])
        zeros = sb("zeros", [P, S])
        WgT = sb("WgT", [P, 2 * CT, D])
        Wn1T = sb("Wn1T", [P, CT, P])
        Wn2T = sb("Wn2T", [P, REP, NT])
        WsT = sb("WsT", [P, CT, D])
        WtT = sb("WtT", [P, CT, D])
        WoT = sb("WoT", [P, CT, D])
        gammaB = sb("gammaB", [P, D])
        betaB = sb("betaB", [P, D])
        bgC = sb("bgC", [P, CT])
        bsC = sb("bsC", [P, CT])
        btC = sb("btC", [P, CT])
        bn1C = sb("bn1C", [P, 1])
        bn2C = sb("bn2C", [P, 1])
        tauC = sb("tauC", [P, 1])
        alphaC = sb("alphaC", [P, 1])
        tauX = sb("tauX", [P, 1])
        alphaX = sb("alphaX", [P, 1])
        decayX = sb("decayX", [P, S])
        blT = sb("blT", [P, CT, NT])
        blM = sb("blM", [P, CT])
        blS = sb("blS", [P, CT])
        blR = sb("blR", [P, CT])
        w4 = sb("w4", [P, CT, REP, NT])
        wrep = sb("wrep", [P, D])
        powers = sb("powers", [P, S + 1])
        rev = sb("rev", [P, S + P])
        before = sb("before", [P, KT, P])
        leave = sb("leave", [P, CS, NT])
        read = sb("read", [P, REP, CH])
        near = sb("near", [P, CH, D], F32R)
        stI = sb("stI", [NSTAGE, B], I32)
        stF = sb("stF", [NSTAGE, B])
        rowI = sb("rowI", [NSTAGE, 1], I32)
        rowF = sb("rowF", [NSTAGE, 1])
        hot = sb("hot", [NSTAGE, B])
        emb = sb("emb", [NSTAGE, S])
        biasR = sb("biasR", [B, S])
        Wgh, Wgl = sb("Wgh", [P, CT, D], F32R), sb("Wgl", [P, CT, D], F32R)
        Wn1h, Wn1l = sb("Wn1h", [P, CT, P], F32R), sb("Wn1l", [P, CT, P], F32R)
        Wsh, Wsl = sb("Wsh", [P, CT, D], F32R), sb("Wsl", [P, CT, D], F32R)
        negHalf = sb("negHalf", [P, NB * ST])
        xn = sb("xn", [P, NB, ST, D])
        kn = sb("kn", [P, NB, ST, D])
        xT = sb("xT", [P, CT, NB, S])
        kT = sb("kT", [P, CT, NB, S])
        bias = sb("bias", [P, NB, S])
        qT = sb("qT", [P, CT, NB, S])
        prob = sb("prob", [P, NB, ST, S])
        x2n = prob
        assert D == S
        probT = sb("probT", [P, ST, NB, S])
        rowmax = sb("rowmax", [P, NB, ST])
        negmax = sb("negmax", [P, NB, ST])
        rowsum = sb("rowsum", [P, NB, ST])
        rowinv = sb("rowinv", [P, NB, ST])
        x2b = sb("x2b", [P, 2, NB, ST, D])
        x2T = sb("x2T", [P, CT, NB, S])
        x2h, x2l = sb("x2h", [P, CT, NB, S], F32R), sb("x2l", [P, CT, NB, S], F32R)
        cxT = sb("cxT", [P, CT, NB, S])
        h1 = sb("h1", [P, N])
        thM = sb("thM", [P, N])
        mN = sb("mN", [P, NB * ST, NT])
        ms = sb("ms", [P, 2, N], F32R)
        th = sb("th", [P, CT, N])
        gT = sb("gT", [P, 2, CT, N])
        gn = sb("gn", [P, NB, ST, D])
        lv = sb("lv", [P, NB, SLOT[ST], NT])
        Hw = sb("Hw", [P, KT, NB, D])
        prod = sb("prod", [P, NPROD, CT, N])
        farN = sb("farN", [P, ST, NB, D])
        farT = sb("farT", [P, CT, N])
        acc = sb("acc", [P, 2, CT, N])
        soma = sb("soma", [P, 2, CT, N])
        sgT = sb("sgT", [P, CT, N])
        stats = sb("stats", [P, NB * ST, 6])
        both = sb("both", [P, NB * ST, 2])
        dif = sb("dif", [P, NB * ST])
        dif2 = sb("dif2", [P, NB * ST])
        mean = sb("mean", [P, NB * ST])
        varE = sb("varE", [P, NB * ST])
        rstd = sb("rstd", [P, NB * ST])
        y = sb("y", [P, 2, NB, ST, D])
        wide = prod[:, :, :, :].rearrange("p i t n -> p (i t n)").rearrange("p (j d) -> p j d", d=D)
        assert NPROD * CT * N == CH * D and CH % NPROD == 0

        nearP = [ctx.enter_context(nc.psum_tensor(f"nearP{i}", [P, CT, N], F32)) for i in range(2)]
        work = [ctx.enter_context(nc.psum_tensor(f"work{i}", [P, 2, N], F32)) for i in range(2)]

        w_in = sem("w_in")
        bias_out = sem("bias_out")
        x_in = sem("x_in")
        k_in = sem("k_in")
        xT_in = sem("xT_in")
        kT_in = sem("kT_in")
        bias_in = sem("bias_in")
        y_out = [sem(f"y_out{i}") for i in range(2)]
        w_late = sem("w_late")
        c_zero = sem("c_zero")
        c_ident, c_row = sem("c_ident"), sem("c_row")
        c_exp, c_blexp = sem("c_exp"), sem("c_blexp")
        c_bias_ps, c_wrep_ps, c_leave_ps = sem("c_bias_ps"), sem("c_wrep_ps"), sem("c_leave_ps")
        c_hot, c_blmax, c_w4 = sem("c_hot"), sem("c_blmax"), sem("c_w4")
        c_biasrow = sem("c_biasrow")
        c_before, c_leave, c_const = sem("c_before"), sem("c_leave"), sem("c_const")
        c_dve = sem("c_dve")
        q_pool = sem("q_pool")
        score_ps = sem("score_ps")
        max_dv, negmax_dv = sem("max_dv"), sem("negmax_dv")
        prob_sb = sem("prob_sb")
        rowinv_dv = sem("rowinv_dv")
        pT_ps, pT_sb = sem("pT_ps"), sem("pT_sb")
        att_ps = sem("att_ps")
        x2_dv = sem("x2_dv")
        x2b_pool = sem("x2b_pool")
        x2T_ps, x2T_sb = sem("x2T_ps"), sem("x2T_sb")
        x2l_dv = sem("x2l_dv")
        cx_dv = sem("cx_dv")
        h1_ps, h1_sb = sem("h1_ps"), sem("h1_sb")
        g_ps, thG_sb, g_dv = sem("g_ps"), sem("thG_sb"), sem("g_dv")
        m_ps, thM_sb, ms_dv = sem("m_ps"), sem("thM_sb"), sem("ms_dv")
        mN_ps, mN_sb = sem("mN_ps"), sem("mN_sb")
        lv_pool = sem("lv_pool")
        gn_ps, gn_sb = sem("gn_ps"), sem("gn_sb")
        st_ps, Hw_dv = sem("st_ps"), sem("Hw_dv")
        farN_ps, farN_sb = sem("farN_ps"), sem("farN_sb")
        far_ps, far_sb = sem("far_ps"), sem("far_sb")
        near_ps, near_dv, near_pool = sem("near_ps"), sem("near_dv"), sem("near_pool")
        far_pool = sem("far_pool")
        soma_ps, soma_sb = sem("soma_ps"), sem("soma_sb")
        tg_ps, tg_sb, sg_dv = sem("tg_ps"), sem("tg_sb"), sem("sg_dv")
        o_ps, o_sb = sem("o_ps"), sem("o_sb")
        st_dv, both_dv, mean_dv, var_dv = sem("st_dv"), sem("both_dv"), sem("mean_dv"), sem("var_dv")
        rstd_pool = sem("rstd_pool")
        cen_dv, y_dv = sem("cen_dv"), sem("y_dv")

        NLOAD = 13 + 2 * REP
        NLATE = 2 + REP
        NZERO = 7

        def need(eng, s, value):
            if not isinstance(value, int) or value > 0:
                eng.wait_ge(s, value)

        def steps(eng, body):
            def peeled(s):
                body(s, s + 2 < PAIRS, s + 1 < PAIRS, 0 <= s < PAIRS, s >= 1, (s + 1) % 2, (s + 1) // 2)

            peeled(-1)
            peeled(0)
            with eng.Fori(0, (PAIRS - 4) // 2) as i:
                body(i * 2 + 1, True, True, True, True, 0, i + 1)
                body(i * 2 + 2, True, True, True, True, 1, i + 1)
            for s in range(PAIRS - 3, PAIRS + 1):
                peeled(s)

        block = ctx.enter_context(nc.Block())

        @block.sync
        def _(sp):
            def load_xT(pair):
                sp.dma_start(xT[:, :, :, :], x_chn[pair]).then_inc(xT_in, 16)

            def load_bias(pair):
                sp.dma_start(bias[:, :, :], bias_d[pair].partition_broadcast(P)).then_inc(bias_in, 16)

            def load_kT(pair):
                sp.dma_start(kT[:, :, :, :], f_chn[pair]).then_inc(kT_in, 16)

            def load_kn(pair):
                sp.dma_start(kn[:, :, :, :], f_pos[pair]).then_inc(k_in, 16)

            def load_xn(pair):
                sp.dma_start(xn[:, :, :, :], x_pos[pair]).then_inc(x_in, 16)

            load_xT(0)
            load_kT(0)
            loads = [
                (stI[:, :], stage.partition_broadcast(NSTAGE)), (emb[:, :], embed),
                (tauX[:, :], tau_ctx.partition_broadcast(P)),
                (blT[:, :, :], blendT.rearrange("(t p) n -> p t n", p=P)),
                (WgT[:, :, :], wgT.rearrange("(t p) n -> p t n", p=P)),
                (WsT[:, :, :], wsT.rearrange("(t p) n -> p t n", p=P)),
                (WtT[:, :, :], wtT.rearrange("(t p) n -> p t n", p=P)),
                (WoT[:, :, :], woT.rearrange("(t p) n -> p t n", p=P)),
                (gammaB[:, :], gamma.partition_broadcast(P)), (betaB[:, :], beta.partition_broadcast(P)),
                (bgC[:, :], bg), (bsC[:, :], bs), (btC[:, :], bt),
            ]
            for dst, src in loads:
                sp.dma_start(dst, src).then_inc(w_in, 16)
            for r in range(REP):
                sp.dma_start(tauC[r * NT:(r + 1) * NT, :], tau.rearrange("(n o) -> n o", o=1)).then_inc(w_in, 16)
                sp.dma_start(bn2C[r * NT:(r + 1) * NT, :], bn2.rearrange("(n o) -> n o", o=1)).then_inc(w_in, 16)
            assert len(loads) + 2 * REP == NLOAD
            sp.wait_ge(c_zero, NZERO)
            sp.dma_start(Wn1T[:, :, 0:NH], wn1T.rearrange("(t p) n -> p t n", p=P)).then_inc(w_late, 16)
            sp.dma_start(bn1C[0:NH, :], bn1.rearrange("(n o) -> n o", o=1)).then_inc(w_late, 16)
            for r in range(REP):
                sp.dma_start(Wn2T[0:NH, r, :], wn2T).then_inc(w_late, 16)
            load_kn(0)
            load_xn(0)
            sp.wait_ge(c_biasrow, 1)
            sp.dma_start(bias_d.rearrange("q b s -> (q b) s"), biasR[:, :]).then_inc(bias_out, 16)
            sp.wait_ge(bias_out, 16)
            load_bias(0)

            def load_next(s):
                need(sp, q_pool, s + 2)
                load_xT(s + 2)
                load_bias(s + 2)
                need(sp, score_ps, (s + 2) * 2)
                load_kT(s + 2)
                need(sp, att_ps, (s + 2) * 2)
                load_kn(s + 2)
                need(sp, x2_dv, (s + 2) * 4)
                load_xn(s + 2)

            def store_last(s, par):
                need(sp, y_dv, s * 4)
                sp.dma_start(out[s - 1], y[:, par]).then_inc(y_out[par], 16)

            load_next(-1)
            load_next(0)
            with sp.Fori(0, (PAIRS - 4) // 2) as i:
                for u in range(2):
                    load_next(i * 2 + 1 + u)
                    store_last(i * 2 + 1 + u, u)
            load_next(PAIRS - 3)
            for s in range(PAIRS - 3, PAIRS + 1):
                store_last(s, (s + 1) % 2)
            for par in range(2):
                sp.wait_ge(y_out[par], 16 * (PAIRS // 2 + 1))

        @block.gpsimd
        def _(pool):
            pool.memset(ident[:, :], 0.0).then_inc(c_zero, 1)
            pool.memset(zeros[:, :], 0.0).then_inc(c_zero, 1)
            pool.memset(Wn1T[:, :, :], 0.0).then_inc(c_zero, 1)
            pool.memset(Wn2T[:, :, :], 0.0).then_inc(c_zero, 1)
            pool.memset(bn1C[:, :], 0.0).then_inc(c_zero, 1)
            pool.memset(read[:, :, :], 0.0).then_inc(c_zero, 1)
            pool.memset(negHalf[:, :], -0.5).then_inc(c_zero, 1)
            pool.wait_ge(c_zero, NZERO)
            pool.affine_select(out=ident[:, :], in_=ident[:, :], compare_op=ALU.not_equal, fill=1.0, base=0,
                               pattern=[[-1, P]], channel_multiplier=1).then_inc(c_ident, 1)
            pool.iota(rowI[:, :], pattern=[[0, 1]], base=0, channel_multiplier=1).then_inc(c_row, 1)
            pool.wait_ge(w_in, 16 * NLOAD)

            def queries(pair):
                need(pool, xT_in, (pair + 1) * 16)
                need(pool, bias_in, (pair + 1) * 16)
                need(pool, score_ps, pair * 2)
                pool.tensor_tensor(qT[:, :, :, :], xT[:, :, :, :],
                                   bias[:, :, :].unsqueeze(1).to_broadcast([P, CT, NB, S]),
                                   ALU.add).then_inc(q_pool, 1)

            queries(0)

            def body(s, n, a, r, z, pa, h):
                pr = 1 - pa

                def add(j):
                    if not r:
                        return
                    need(pool, near_dv, s * CH + j + 1)
                    if j == FAR_AFTER + 1:
                        need(pool, far_pool, s + 1)
                    elif j > 1:
                        need(pool, near_pool, s * NADD + j - 1)
                    d = acc[:, pr].rearrange("p t (c k) -> p t c k", k=CH)[:, :, :, j:CH]
                    src = prod[:, j % NPROD, :, 0:CHN * (CH - j)].rearrange("p t (c k) -> p t c k", k=CH - j)
                    pool.tensor_tensor(d, d, src, ALU.add).then_inc(near_pool, 1)
                    if j == FAR_AFTER:
                        need(pool, far_sb, (s + 1) * 2)
                        need(pool, near_pool, s * NADD + j)
                        pool.tensor_tensor(acc[:, pr], acc[:, pr], farT[:, :, :], ALU.add)\
                            .then_inc(far_pool, 1)

                for j in range(1, 5):
                    add(j)
                if n:
                    queries(s + 2)
                for j in range(5, 8):
                    add(j)
                if z:
                    tail(s)
                for j in range(8, 10):
                    add(j)
                if a:
                    need(pool, x2_dv, (s + 2) * 4)
                    if z:
                        need(pool, y_dv, s * 4)
                    bb = betaB[:, :].unsqueeze(1).to_broadcast([P, NB * ST, D])
                    pool.tensor_tensor(x2b[:, pa].rearrange("p b t d -> p (b t) d"),
                                       x2n[:, :, :, :].rearrange("p b t d -> p (b t) d"), bb,
                                       ALU.add).then_inc(x2b_pool, 1)
                for j in range(10, CH):
                    add(j)
                if a:
                    if not r:
                        pool.wait_ge(c_leave, 1)
                    need(pool, mN_sb, s + 2)
                    if r:
                        need(pool, st_ps, (s + 1) * 4)
                    for t in range(ST):
                        n = SLOT[t + 1] - SLOT[t]
                        each = [P, NB, n, NT]
                        pool.tensor_tensor(
                            lv[:, :, SLOT[t]:SLOT[t + 1], :],
                            mN[:, :, :].rearrange("p (b t) n -> p b t n", t=ST)[:, :, t, :].unsqueeze(2)
                            .to_broadcast(each),
                            leave[:, 0:n, :].unsqueeze(1).to_broadcast(each), ALU.mult).then_inc(lv_pool, 1)

            def tail(s):
                need(pool, var_dv, s)
                pool.tensor_tensor(rstd[:, :], varE[:, :], negHalf[:, :], ALU.pow).then_inc(rstd_pool, 1)

            steps(pool, body)

        @block.scalar
        def _(act):
            act.wait_ge(w_in, 16 * NLOAD)
            act.activation(alphaC[:, :], tauC[:, :], ACT.Exp).then_inc(c_exp, 1)
            act.activation(alphaX[:, :], tauX[:, :], ACT.Exp).then_inc(c_exp, 1)
            act.wait_ge(c_blmax, 1)
            for t in range(CT):
                act.activation(blT[:, t, :], blT[:, t, :], ACT.Exp, bias=blM[:, t:t + 1],
                               accum_out=blS[:, t:t + 1]).then_inc(c_blexp, 1)
            act.wait_ge(c_const, 1)

            def body(s, n, a, r, z, pa, h):
                pr = 1 - pa
                def exps(b):
                    need(act, negmax_dv, (s + 1) * 2 + b + 1)
                    if b == 0 and r:
                        need(act, rowinv_dv, s + 1)
                        need(act, x2b_pool, s + 1)
                    for t in range(ST):
                        act.activation(prob[:, b, t, :], work[0][:, b, t * S:(t + 1) * S], ACT.Exp,
                                       bias=negmax[:, b, t:t + 1],
                                       accum_out=rowsum[:, b, t:t + 1]).then_inc(prob_sb, 1)

                if a:
                    exps(0)
                if r:
                    for b in range(NB):
                        need(act, gn_ps, s * 2 + b + 1)
                        act.copy(gn[:, b].rearrange("p t d -> p (t d)"), work[1][:, b, :]).then_inc(gn_sb, 1)
                if a:
                    exps(1)
                if z:
                    for t in range(CT):
                        need(act, tg_ps, (s - 1) * 2 + t + 1)
                        if t == 0 and r:
                            need(act, g_dv, (s + 1) * 2)
                        act.activation(th[:, t, :], work[1][:, t, :], ACT.Tanh, bias=btC[:, t:t + 1],
                                       scale=0.5).then_inc(tg_sb, 1)
                if a:
                    for t in range(ST):
                        need(act, pT_ps, (s + 1) * 2 + t + 1)
                        act.copy(probT[:, t].rearrange("p b s -> p (b s)"), work[0][:, t, :]).then_inc(pT_sb, 1)
                if r:
                    for t in range(CT):
                        need(act, soma_ps, s * 2 + t + 1)
                        act.activation(soma[:, pr, t, :], work[1][:, t, :], ACT.Gelu,
                                       bias=bsC[:, t:t + 1]).then_inc(soma_sb, 1)
                if r:
                    for t in range(ST):
                        need(act, farN_ps, s * 2 + t + 1)
                        act.copy(farN[:, t].rearrange("p b d -> p (b d)"), work[1][:, t, :]).then_inc(farN_sb, 1)
                if a:
                    for t in range(CT):
                        need(act, x2T_ps, (s + 1) * 2 + t + 1)
                        act.copy(x2h[:, t].rearrange("p b s -> p (b s)"), work[0][:, t, :])
                        act.copy(x2T[:, t].rearrange("p b s -> p (b s)"), work[0][:, t, :]).then_inc(x2T_sb, 1)
                if r:
                    for t in range(CT):
                        need(act, far_ps, s * 2 + t + 1)
                        if t == 0:
                            need(act, far_pool, s)
                        act.copy(farT[:, t, :], work[1][:, t, :]).then_inc(far_sb, 1)
                if z:
                    for b in range(NB):
                        need(act, o_ps, (s - 1) * 2 + b + 1)
                        if b == 0:
                            need(act, y_out[pa], h * 16)
                        act.copy(y[:, pa, b].rearrange("p t d -> p (t d)"),
                                 work[1][:, b, :]).then_inc(o_sb, 1)
                if a:
                    need(act, h1_ps, s + 2)
                    act.activation(h1[:, :], work[0][:, 0, :], ACT.Gelu, bias=bn1C[:, 0:1]).then_inc(h1_sb, 1)
                if a:
                    for t in range(CT):
                        need(act, g_ps, (s + 1) * 2 + t + 1)
                        if t == 0 and z:
                            need(act, sg_dv, s * 2)
                        act.activation(th[:, t, :], work[1][:, t, :], ACT.Tanh, bias=bgC[:, t:t + 1],
                                       scale=0.5).then_inc(thG_sb, 1)
                        if t == 0:
                            need(act, m_ps, s + 2)
                            act.activation(thM[:, :], work[0][:, 0, :], ACT.Tanh, bias=bn2C[:, 0:1],
                                           scale=0.5).then_inc(thM_sb, 1)
                    need(act, mN_ps, s + 2)
                    if r:
                        need(act, lv_pool, (s + 1) * ST)
                    act.activation(mN[:, :, :], work[0][:, 1, :].rearrange("p (q n) -> p q n", n=P)[:, :, 0:NT],
                                   ACT.Copy, bias=2.0).then_inc(mN_sb, 1)

            steps(act, body)

        @block.tensor
        def _(pe):
            pe.wait_ge(c_ident, 1)
            pe.wait_ge(c_hot, 1)
            pe.matmul(work[0][0:B, 0, 0:S], hot[:, :], emb[:, :], start=True, stop=True).then_inc(c_bias_ps, 1)
            pe.wait_ge(c_w4, 1)
            for t in range(CT):
                ins = pe.transpose(work[1][:, 0, t * P:(t + 1) * P],
                                   w4[:, t].rearrange("p r n -> p (r n)"), ident[:, :])
            ins.then_inc(c_wrep_ps, 1)
            pe.wait_ge(c_before, 1)
            for m in range(KT):
                ins = pe.transpose(work[1][:, 1, m * P:(m + 1) * P], before[:, m, :], ident[:, :])
            ins.then_inc(c_leave_ps, 1)
            pe.wait_ge(c_const, 1)

            def transposes(dst, src_of, done):
                for t in range(2):
                    for i in range(N // P):
                        ins = pe.transpose(dst[:, t, i * P:(i + 1) * P], src_of(t, i), ident[:, :])
                    ins.then_inc(done, 1)

            def project(dst, weights, parts, done, free):
                for e in range(CT):
                    free(e)
                    for k, part in enumerate(parts):
                        ins = pe.matmul(dst[:, e, :], weights[:, k, e * P:(e + 1) * P], part,
                                        start=(k == 0), stop=(k == len(parts) - 1))
                    ins.then_inc(done, 1)

            def thrice(dst, lh, ll, rh, rl, first, last):
                pe.matmul(dst, lh, rh, start=first, stop=False)
                pe.matmul(dst, ll, rh, start=False, stop=False)
                return pe.matmul(dst, lh, rl, start=False, stop=last)

            def flat(v, k):
                return v[:, k].rearrange("p b s -> p (b s)")

            def body(s, n, a, r, z, pa, h):
                pr = 1 - pa

                def near_group(g):
                    if not r:
                        return
                    p = nearP[g % 2]
                    if g == 0:
                        need(pe, ms_dv, (s + 1) * 2)
                    last = GROUPS[g - 2][-1] + 1 if g >= 2 else GROUPS[NG - 2 + g][-1] + 1 - CH
                    need(pe, near_dv, s * CH + last)
                    for t in range(CT):
                        at = 0
                        for j in GROUPS[g]:
                            k = width(j)
                            ins = pe.matmul(p[:, t, at:at + CHN * k], near[:, j, t * P:(t + 1) * P],
                                            ms[:, pr, :].rearrange("p (c k) -> p c k", k=CH)[:, :, 0:k],
                                            start=True, stop=True)
                            at += CHN * k
                    ins.then_inc(near_ps, 1)

                def states(b, free):
                    for m in range(KT):
                        if m % 2 == 0:
                            free(m // 2)
                        tiles = m * REP * CH // P + 1
                        for t in range(tiles):
                            at = SLOT[t] + m * REP - t * (P // CH)
                            ins = pe.matmul(work[1][:, m // 2, (m % 2) * D:(m % 2 + 1) * D],
                                            lv[:, b, at:at + REP, :].rearrange("p c n -> p (c n)"),
                                            gn[:, b, t, :], start=(t == 0), stop=(t == tiles - 1))
                        if m % 2:
                            ins.then_inc(st_ps, 1)

                if a:
                    need(pe, q_pool, s + 2)
                    need(pe, kT_in, (s + 2) * 16)
                    for b in range(NB):
                        if r:
                            need(pe, mN_sb if b else thM_sb, s + 1)
                        for t in range(ST):
                            for k in range(CT):
                                ins = pe.matmul(work[0][:, b, t * S:(t + 1) * S],
                                                qT[:, k, b, t * P:(t + 1) * P], kT[:, k, b, :],
                                                start=(k == 0), stop=(k == CT - 1))
                        ins.then_inc(score_ps, 1)
                if r:
                    need(pe, g_dv, (s + 1) * 2)
                    for b in range(NB):
                        for t in range(ST):
                            for k in range(CT):
                                ins = pe.transpose(work[1][:, b, t * D + k * P:t * D + (k + 1) * P],
                                                   gT[:, pr, k, b * S + t * P:b * S + (t + 1) * P], ident[:, :])
                        ins.then_inc(gn_ps, 1)
                near_group(0)
                near_group(1)
                if z:
                    need(pe, near_pool, s * NADD)
                    if not r:
                        need(pe, o_sb, (s - 1) * 2)
                    project(work[1], WtT, [acc[:, pa, k, :] for k in range(CT)], tg_ps,
                            lambda e: r and need(pe, gn_sb, s * 2 + e + 1))
                near_group(2)
                if a:
                    need(pe, prob_sb, (s + 2) * 4)
                    transposes(work[0], lambda t, i: prob[:, i // ST, i % ST, t * P:(t + 1) * P], pT_ps)
                if r:
                    need(pe, lv_pool, (s + 1) * ST)
                    need(pe, gn_sb, (s + 1) * 2)
                    states(0, lambda k: z and need(pe, tg_sb, (s - 1) * 2 + k + 1))
                near_group(3)
                if a:
                    need(pe, pT_sb, (s + 2) * 2)
                    need(pe, k_in, (s + 2) * 16)
                    for b in range(NB):
                        for t in range(ST):
                            for k in range(ST):
                                ins = pe.matmul(work[0][:, b, t * D:(t + 1) * D],
                                                probT[:, k, b, t * P:(t + 1) * P], kn[:, b, k, :],
                                                start=(k == 0), stop=(k == ST - 1))
                        ins.then_inc(att_ps, 1)
                if r:
                    states(1, lambda k: need(pe, Hw_dv, s * 4 + k + 1))
                near_group(4)
                if r:
                    for e in range(CT):
                        need(pe, Hw_dv, s * 4 + 2 + e + 1)
                        cols = slice(e * P, (e + 1) * P)
                        for k in range(CT):
                            ins = thrice(work[1][:, e, :], Wsh[:, k, cols], Wsl[:, k, cols], flat(x2h, k),
                                         flat(x2l, k), k == 0, k == CT - 1)
                        ins.then_inc(soma_ps, 1)
                near_group(5)
                if r:
                    for m in range(KT):
                        rows = slice(m * REP * CH % P, m * REP * CH % P + REP * CH)
                        if rows.start == 0:
                            need(pe, soma_sb, s * 2 + m * REP * CH // P + 1)
                        ins = pe.matmul(work[1][rows, m * REP * CH // P, :], read[:, :, :].rearrange("p c k -> p (c k)"),
                                        Hw[:, m, :, :].rearrange("p b d -> p (b d)"), start=True, stop=True)
                        if rows.stop == P:
                            ins.then_inc(farN_ps, 1)
                if a:
                    need(pe, x2_dv, (s + 2) * 4)
                    transposes(work[0], lambda t, i: x2n[:, i // ST, i % ST, t * P:(t + 1) * P], x2T_ps)
                near_group(6)
                if r:
                    need(pe, farN_sb, (s + 1) * 2)
                    transposes(work[1], lambda t, i: farN[:, i % ST, i // ST, t * P:(t + 1) * P], far_ps)
                near_group(7)
                if z:
                    need(pe, sg_dv, s * 2)
                    for b in range(NB):
                        if r:
                            need(pe, far_sb, s * 2 + b + 1)
                        for t in range(ST):
                            for k in range(CT):
                                ins = pe.matmul(work[1][:, b, t * D:(t + 1) * D],
                                                sgT[:, k, b * S + t * P:b * S + (t + 1) * P], WoT[:, k, :],
                                                start=(k == 0), stop=(k == CT - 1))
                        ins.then_inc(o_ps, 1)
                if a:
                    need(pe, x2T_sb, (s + 2) * 2)
                    need(pe, x2l_dv, (s + 2) * 2)
                    for k in range(CT):
                        ins = thrice(work[0][:, 0, :], Wn1h[:, k, :], Wn1l[:, k, :], flat(x2h, k),
                                     flat(x2l, k), k == 0, k == CT - 1)
                    ins.then_inc(h1_ps, 1)
                near_group(8)
                if a:
                    if r and not z:
                        need(pe, far_sb, (s + 1) * 2)
                for e in range(CT):
                    if a:
                        cols = slice(e * P, (e + 1) * P)
                        if z:
                            need(pe, o_sb, (s - 1) * 2 + e + 1)
                        for k in range(CT):
                            thrice(work[1][:, e, :], Wgh[:, k, cols], Wgl[:, k, cols], flat(x2h, k),
                                   flat(x2l, k), k == 0, False)
                        if e == 0:
                            need(pe, cx_dv, (s + 2) * 4)
                        for k in range(CT):
                            ins = pe.matmul(work[1][:, e, :], WgT[:, CT + k, cols], flat(cxT, k),
                                            start=False, stop=(k == CT - 1))
                        ins.then_inc(g_ps, 1)
                    if e == 0:
                        near_group(9)
                    if a and e == 0:
                        need(pe, h1_sb, s + 2)
                        pe.matmul(work[0][:, 0, :], Wn2T[:, :, :].rearrange("p r n -> p (r n)"), h1[:, :],
                                  start=True, stop=True).then_inc(m_ps, 1)
                if a:
                    need(pe, thM_sb, s + 2)
                    for i in range(N // P):
                        ins = pe.transpose(work[0][:, 1, i * P:(i + 1) * P], thM[:, i * P:(i + 1) * P],
                                           ident[:, :])
                    ins.then_inc(mN_ps, 1)
                near_group(10)
                near_group(11)

            steps(pe, body)

        @block.vector
        def _(dve):
            chain = [0]

            def link(ins):
                chain[0] += 1
                ins.then_inc(c_dve, 1)
                dve.wait_ge(c_dve, chain[0])

            dve.wait_ge(w_in, 16 * NLOAD)
            dve.wait_ge(c_row, 1)
            link(dve.tensor_copy(stF[:, :], stI[:, :]))
            link(dve.tensor_copy(rowF[:, :], rowI[:, :]))
            dve.tensor_scalar(hot[:, :], stF[:, :], rowF[:, 0:1], None, ALU.is_equal).then_inc(c_hot, 1)
            link(dve.tensor_reduce(blM[:, :], blT[:, :, :], AX_X, ALU.max))
            dve.tensor_scalar(blM[:, :], blM[:, :], -1.0, None, ALU.mult).then_inc(c_blmax, 1)
            dve.wait_ge(c_exp, 2)
            for a_ in (alphaC, alphaX):
                link(dve.tensor_scalar(a_[:, :], a_[:, :], 1.0, None, ALU.add))
                link(dve.reciprocal(a_[:, :], a_[:, :]))
            dve.wait_ge(c_zero, NZERO)
            dve.tensor_scalar(decayX[:, :], zeros[:, :], alphaX[:, 0:1], None, ALU.add)
            dve.memset(powers[:, 0:1], 1.0)
            link(dve.tensor_tensor_scan(powers[:, 1:S + 1], alphaC[:, 0:1].to_broadcast([P, S]), zeros[:, :],
                                        1.0, ALU.mult, ALU.add))
            dve.memset(rev[:, S:], 0.0)
            link(dve.tensor_copy(rev[:, 0:S], powers[:, 0:S][:, ::-1]))
            for c in range(CS):
                rows, m = slice(c % REP * NT, (c % REP + 1) * NT), c // REP
                ins = dve.tensor_copy(before[rows, m, :], rev[rows, S - c * CH:S - c * CH + P])
            ins.then_inc(c_before, 1)
            dve.wait_ge(c_blexp, CT)
            link(dve.reciprocal(blR[:, :], blS[:, :]))
            for t in range(CT):
                for r in range(REP):
                    ins = dve.tensor_scalar(w4[:, t, r, :], blT[:, t, :], blR[:, t:t + 1], 0.25,
                                            ALU.mult, ALU.mult)
            ins.then_inc(c_w4, 1)
            for r in range(REP):
                dve.tensor_copy(read[r * NT:(r + 1) * NT, r, :], powers[r * NT:(r + 1) * NT, 1:1 + CH])
            dve.wait_ge(c_bias_ps, 1)
            dve.tensor_copy(biasR[:, :], work[0][0:B, 0, 0:S]).then_inc(c_biasrow, 1)
            dve.wait_ge(c_wrep_ps, 1)
            link(dve.tensor_copy(wrep[:, :], work[1][:, 0, 0:D]))
            dve.wait_ge(c_leave_ps, 1)
            dve.tensor_copy(leave[:, :, :], work[1][:, 1, :].rearrange("p (c n) -> p c n", n=NT))\
               .then_inc(c_leave, 1)
            for j in range(CH):
                ins = dve.tensor_scalar(wide[:, j, :], wrep[:, :], powers[:, j:j + 1], None, ALU.mult)
            link(ins)
            link(dve.tensor_copy(near[:, :, :], wide))
            for r in range(1, REP, 2):
                rows = slice(r * NT, (r + 1) * NT)
                dve.tensor_tensor(near[rows], wide[rows], near[rows].bitcast(F32), ALU.subtract)
            for v in (bgC, btC, bn2C):
                dve.tensor_scalar(v[:, :], v[:, :], 0.5, None, ALU.mult)
            link(dve.tensor_scalar(WoT[:, :, :], WoT[:, :, :], 0.5, None, ALU.mult))
            dve.wait_ge(w_late, 16 * NLATE)
            for w, hi, lo in ((WgT[:, 0:CT, :], Wgh, Wgl), (Wn1T[:, :, :], Wn1h, Wn1l), (WsT[:, :, :], Wsh, Wsl)):
                link(dve.tensor_copy(hi[:, :, :], w))
                ins = dve.tensor_tensor(lo[:, :, :], w, hi[:, :, :].bitcast(F32), ALU.subtract)
            ins.then_inc(c_const, 1)
            for par in range(2):
                dve.memset(y[:, par, 0, 0, 0:1], 0.0).then_inc(y_out[par], 16)

            def body(s, n, a, r, z, pa, h):
                def near_group(g):
                    if not r:
                        return
                    need(dve, near_ps, s * NG + g + 1)
                    at = 0
                    for j in GROUPS[g]:
                        n, m = width(j), CH - j
                        src = nearP[g % 2][:, :, at:at + CHN * n].rearrange("p t (c k) -> p t c k", k=n)
                        gv = gT[:, 1 - pa].rearrange("p t (c k) -> p t c k", k=CH)
                        dst = prod[:, j % NPROD, :, 0:CHN * m].rearrange("p t (c k) -> p t c k", k=m)
                        if j == 0:
                            dst = acc[:, 1 - pa].rearrange("p t (c k) -> p t c k", k=CH)
                        else:
                            need(dve, near_pool, s * NADD + (j - NPROD if j >= NPROD else j - NPROD + 1))
                        dve.tensor_tensor(dst, src[:, :, :, 0:m], gv[:, :, :, 0:m], ALU.mult)\
                           .then_inc(near_dv, 1)
                        at += CHN * n

                def gate(t):
                    need(dve, thG_sb, (s + 1) * 2 + t + 1)
                    if t == 0 and r:
                        need(dve, gn_ps, s * 2)
                    dve.scalar_tensor_tensor(out=gT[:, pa, t, :], in0=th[:, t, :], scalar=1.0,
                                             in1=x2T[:, t].rearrange("p b s -> p (b s)"),
                                             op0=ALU.add, op1=ALU.mult).then_inc(g_dv, 1)

                def weigh_states(b):
                    for k in range(2):
                        need(dve, st_ps, s * 4 + 2 * b + k + 1)
                        dve.tensor_tensor(
                            Hw[:, 2 * k:2 * k + 2, b, :],
                            work[1][:, k, :].rearrange("p (m d) -> p m d", d=D),
                            wrep[:, :].unsqueeze(1).to_broadcast([P, 2, D]), ALU.mult).then_inc(Hw_dv, 1)

                if a:
                    for b in range(NB):
                        need(dve, score_ps, (s + 1) * 2 + b + 1)
                        dve.tensor_reduce(rowmax[:, b, :], work[0][:, b, :].rearrange("p (t s) -> p t s", s=S),
                                          AX_X, ALU.max).then_inc(max_dv, 1)
                        need(dve, max_dv, (s + 1) * 2 + b + 1)
                        dve.tensor_scalar(negmax[:, b, :], rowmax[:, b, :], -1.0, None, ALU.mult)\
                           .then_inc(negmax_dv, 1)
                near_group(0)
                near_group(1)
                if z:
                    for t in range(CT):
                        need(dve, tg_sb, (s - 1) * 2 + t + 1)
                        dve.scalar_tensor_tensor(out=sgT[:, t, :], in0=th[:, t, :], scalar=1.0,
                                                 in1=soma[:, pa, t, :], op0=ALU.add, op1=ALU.mult)\
                           .then_inc(sg_dv, 1)
                near_group(2)
                if r:
                    weigh_states(0)
                if a:
                    need(dve, prob_sb, (s + 2) * 4)
                    dve.reciprocal(rowinv[:, :, :], rowsum[:, :, :]).then_inc(rowinv_dv, 1)
                near_group(3)
                if r:
                    weigh_states(1)
                near_group(4)
                if a:
                    need(dve, rowinv_dv, s + 2)
                    need(dve, x_in, (s + 2) * 16)
                    if r:
                        need(dve, x2b_pool, s + 1)
                    for b in range(NB):
                        need(dve, att_ps, (s + 1) * 2 + b + 1)
                        for t in range(ST):
                            dve.scalar_tensor_tensor(
                                out=x2n[:, b, t, :], in0=work[0][:, b, t * D:(t + 1) * D],
                                scalar=rowinv[:, b, t:t + 1], in1=xn[:, b, t, :],
                                op0=ALU.mult, op1=ALU.add).then_inc(x2_dv, 1)
                near_group(5)
                near_group(6)
                if a:
                    for k in range(CT):
                        need(dve, x2T_sb, (s + 1) * 2 + k + 1)
                        dve.tensor_tensor(x2l[:, k, :, :], x2T[:, k, :, :], x2h[:, k, :, :].bitcast(F32),
                                          ALU.subtract).then_inc(x2l_dv, 1)
                    for k in range(CT):
                        for b in range(NB):
                            dve.tensor_tensor_scan(cxT[:, k, b, :], decayX[:, :], x2T[:, k, b, :], 0.0,
                                                   ALU.mult, ALU.add).then_inc(cx_dv, 1)
                near_group(7)
                if z:
                    for q in range(NB * ST):
                        b, t = q // ST, q % ST
                        if t == 0:
                            need(dve, o_sb, (s - 1) * 2 + b + 1)
                        dve.bn_stats(stats[:, q, :], y[:, pa, b, t, :]).then_inc(st_dv, 1)
                    need(dve, st_dv, s * 4)
                    dve.tensor_tensor(both[:, :, :], stats[:, :, 1:3], stats[:, :, 4:6], ALU.add)\
                       .then_inc(both_dv, 1)
                    dve.tensor_tensor(dif[:, :], stats[:, :, 1], stats[:, :, 4], ALU.subtract)\
                       .then_inc(both_dv, 1)
                    need(dve, both_dv, s * 2)
                    dve.tensor_scalar(mean[:, :], both[:, :, 0], 0.5, None, ALU.mult).then_inc(mean_dv, 1)
                    dve.tensor_tensor(dif2[:, :], dif[:, :], dif[:, :], ALU.mult).then_inc(mean_dv, 1)
                    dve.tensor_scalar(varE[:, :], both[:, :, 1], 1.0 / D, EPS, ALU.mult, ALU.add)\
                       .then_inc(mean_dv, 1)
                    need(dve, mean_dv, s * 3)
                    dve.scalar_tensor_tensor(out=varE[:, :], in0=dif2[:, :], scalar=0.25, in1=varE[:, :],
                                             op0=ALU.mult, op1=ALU.add).then_inc(var_dv, 1)
                    for q in range(NB * ST):
                        v = y[:, pa, q // ST, q % ST, :]
                        dve.scalar_tensor_tensor(
                            out=v, in0=v, scalar=mean[:, q:q + 1],
                            in1=gammaB[:, :], op0=ALU.subtract, op1=ALU.mult).then_inc(cen_dv, 1)
                near_group(8)
                near_group(9)
                if a:
                    gate(0)
                if z:
                    need(dve, rstd_pool, s)
                    need(dve, x2b_pool, s)
                    need(dve, cen_dv, s * 4)
                    for q in range(NB * ST):
                        v = y[:, pa, q // ST, q % ST, :]
                        dve.scalar_tensor_tensor(
                            out=v, in0=v, scalar=rstd[:, q:q + 1],
                            in1=x2b[:, pa, q // ST, q % ST, :], op0=ALU.mult, op1=ALU.add).then_inc(y_dv, 1)
                if a:
                    need(dve, thM_sb, s + 2)
                    dve.tensor_scalar(ms[:, pa, :], thM[:, :], 2.0, None, ALU.add).then_inc(ms_dv, 1)
                    need(dve, ms_dv, (s + 1) * 2 + 1)
                    up = slice(P // 2, P)
                    dve.scalar_tensor_tensor(out=ms[up, pa, :], in0=thM[up, :], scalar=2.0,
                                             in1=ms[up, pa, :].bitcast(F32), op0=ALU.add, op1=ALU.subtract)\
                       .then_inc(ms_dv, 1)
                near_group(10)
                if a:
                    gate(1)
                near_group(11)

            steps(dve, body)


def kernel(x, fside_BxSxS_0, itok_B_0_5, condB_tauraws, cond_256, condB_bn2, cond_1024, L0_cond_braak_embed,
           L1_cond_tau_ctx, L1_cond_Wg, L1_cond_bg, L1_cond_Wn1, L1_cond_bn1, L1_cond_Wsoma, L1_cond_bsoma,
           L1_cond_Wtemp, L1_cond_btemp, L1_cond_Wout, L1_cond_gamma, L1_cond_beta):
    import numpy as np
    import concourse.bacc as bacc
    from concourse.bass_utils import run_bass_kernel_spmd

    def by_partition(v):
        return np.asarray(v).reshape(-1, P).T

    B, S, D = x.shape
    NB = 2

    def by_position(v):
        return np.asarray(v).reshape(B // NB, NB, S // P, P, D).transpose(0, 3, 1, 2, 4)

    def by_channel(v):
        return np.asarray(v).reshape(B // NB, NB, S, D // P, P).transpose(0, 4, 3, 1, 2)

    arrays = {
        "x_pos": by_position(x), "f_pos": by_position(fside_BxSxS_0),
        "x_chn": by_channel(x), "f_chn": by_channel(fside_BxSxS_0), "stage": itok_B_0_5, "tau": condB_tauraws,
        "wn2T": np.asarray(cond_256).T, "bn2": condB_bn2, "blendT": np.asarray(cond_1024).T,
        "embed": L0_cond_braak_embed, "tau_ctx": np.asarray(L1_cond_tau_ctx).reshape(1),
        "wgT": np.asarray(L1_cond_Wg).T, "bg": by_partition(L1_cond_bg), "wn1T": np.asarray(L1_cond_Wn1).T,
        "bn1": L1_cond_bn1, "wsT": np.asarray(L1_cond_Wsoma).T, "bs": by_partition(L1_cond_bsoma),
        "wtT": np.asarray(L1_cond_Wtemp).T, "bt": by_partition(L1_cond_btemp), "woT": np.asarray(L1_cond_Wout).T,
        "gamma": L1_cond_gamma, "beta": L1_cond_beta,
    }
    arrays = {"in_" + k: np.ascontiguousarray(v) for k, v in arrays.items()}
    nc = bacc.Bacc("TRN2", target_bir_lowering=False, num_devices=1)
    args = [nc.dram_tensor(k, v.shape, mybir.dt.from_np(v.dtype), kind="ExternalInput").ap()
            for k, v in arrays.items()]
    out = nc.dram_tensor("out", arrays["in_x_pos"].shape, F32, kind="ExternalOutput").ap()
    build(nc, *args, out)
    got = run_bass_kernel_spmd(nc, [arrays], core_ids=[0]).results[0]["out"]
    return got.transpose(0, 2, 3, 1, 4).reshape(B, S, D)
```

```python
from contextlib import ExitStack

import concourse.bass as bass
from concourse import mybir

F32 = mybir.dt.float32
F32R = mybir.dt.float32r
I32 = mybir.dt.int32
ALU = mybir.AluOpType
ACT = mybir.ActivationFunctionType
AX_X = mybir.AxisListType.X

P = 128


def build(nc, x_pos, f_pos, x_chn, f_chn, stage, embed, blend, columns, rows, wn2, weights, out):
    PAIRS, _, NB, ST, D = x_pos.shape
    _, _, CT, _, S = x_chn.shape
    B = PAIRS * NB
    NT = blend.shape[2]
    NSTAGE = embed.shape[0]
    CH = 16
    REP = P // NT
    KT = S // (REP * CH)
    N = NB * S
    CHN = N // CH
    CS = P // CH
    assert ST == 2
    EPS = 1e-5
    HC = CH // 2
    GROUPS = [(j,) for j in range(HC)] + [(j, j + 1) for j in range(HC, CH, 2)]
    NG = len(GROUPS)

    def width(j):
        return max((CH - j + 1) // 2 * 2, HC)

    NPROD = 4
    NADD = CH - 1
    FAR_AFTER = 9

    bias_d = nc.dram_tensor("bias_rows", (PAIRS, NB, S), F32, kind="Internal").ap()

    with ExitStack() as ctx:
        def sb(name, shape, dt=F32):
            return ctx.enter_context(nc.sbuf_tensor(name, shape, dt))

        def sem(name):
            return ctx.enter_context(nc.semaphore(name))

        WC = weights.shape[1]
        WH, WL = sb("WH", [P, WC], F32R), sb("WL", [P, WC], F32R)

        def packed(at, tiles, n):
            return [w[:, at:at + tiles * n].rearrange("p (t n) -> p t n", n=n) for w in (WH, WL)]

        Wg = packed(0, 2 * CT, D)
        Ws = packed(2 * CT * D, CT, D)
        Wt = packed(3 * CT * D, CT, D)
        Wo = packed(4 * CT * D, CT, D)
        Wn1 = packed(5 * CT * D, CT, P)
        assert WC == 5 * CT * D + CT * P
        cols = sb("cols", [P, columns.shape[1]])
        bgC, bsC, btC = (cols[:, i * CT:(i + 1) * CT] for i in range(3))
        bn1C, bn2C, tauC, tauX = (cols[:, 3 * CT + i:3 * CT + i + 1] for i in range(4))
        Wn2 = sb("Wn2", [P, REP * NT])
        ident = sb("ident", [P, P])
        gamma_beta = sb("gamma_beta", [P, 2, D])
        gammaB, betaB = gamma_beta[:, 0, :], gamma_beta[:, 1, :]
        alphaC = sb("alphaC", [P, 1])
        alphaX = sb("alphaX", [P, 1])
        blM = sb("blM", [P, CT])
        blS = sb("blS", [P, CT])
        blR = sb("blR", [P, CT])
        wrep = sb("wrep", [P, D])
        leave = sb("leave", [P, CS, NT])
        read = sb("read", [P, 2, REP, CH])
        carry = sb("carry", [P, P])
        near = sb("near", [P, CH, D], F32R)
        stI = sb("stI", [NSTAGE, B], I32)
        stF = sb("stF", [NSTAGE, B])
        rowI = sb("rowI", [NSTAGE, 1], I32)
        rowF = sb("rowF", [NSTAGE, 1])
        hot = sb("hot", [NSTAGE, B])
        negHalf = sb("negHalf", [P, NB * ST])
        xn = sb("xn", [P, NB, ST, D])
        kn = sb("kn", [P, NB, ST, D])
        knh, knl = sb("knh", [P, NB, ST, D], F32R), sb("knl", [P, NB, ST, D], F32R)
        xT = sb("xT", [P, CT, NB, S])
        kT = sb("kT", [P, CT, NB, S])
        bias = sb("bias", [P, NB, S])
        qT = xT
        kTh, kTl = sb("kTh", [P, CT, NB, S], F32R), sb("kTl", [P, CT, NB, S], F32R)
        prob = sb("prob", [P, NB, ST, S])
        x2n = sb("x2n", [P, NB, ST, D])
        rowmax = sb("rowmax", [P, NB, ST])
        negmax = sb("negmax", [P, NB, ST])
        rowsum = sb("rowsum", [P, NB, ST])
        rowinv = sb("rowinv", [P, NB, ST])
        x2b = sb("x2b", [P, 2, NB, ST, D])
        x2T = sb("x2T", [P, CT, NB, S])
        x2h, x2l = sb("x2h", [P, CT, NB, S], F32R), sb("x2l", [P, CT, NB, S], F32R)
        cxT = sb("cxT", [P, CT, NB, S])
        cxh, cxl = sb("cxh", [P, CT, NB, S], F32R), sb("cxl", [P, CT, NB, S], F32R)
        probTh, probTl = cxh, cxl
        assert CT == ST
        mN = sb("mN", [P, NB * ST, NT])
        ms = sb("ms", [P, 2, N], F32R)
        th = sb("th", [P, CT, N])
        gT = sb("gT", [P, 2, CT, N])
        gn = sb("gn", [P, NB, ST, D])
        lv = sb("lv", [P, NB * ST, CS, NT])
        Hw = sb("Hw", [P, KT, NB, D])
        prod = sb("prod", [P, NPROD, CT, N])
        farN = sb("farN", [P, ST, NB, D])
        h1, thM = (farN[:, i].rearrange("p b d -> p (b d)") for i in range(2))
        assert ST == 2 and D == S
        farT = sb("farT", [P, CT, N])
        acc = sb("acc", [P, 2, CT, N])
        tailh, taill = sb("tailh", [P, CT, N], F32R), sb("taill", [P, CT, N], F32R)
        qh, ql = (v[:, :, :].rearrange("p k (b s) -> p k b s", s=S) for v in (tailh, taill))
        soma = sb("soma", [P, 2, CT, N])
        stats = sb("stats", [P, NB * ST, 6])
        both = sb("both", [P, NB * ST, 2])
        dif = sb("dif", [P, NB * ST])
        dif2 = sb("dif2", [P, NB * ST])
        mean = sb("mean", [P, NB * ST])
        varE = sb("varE", [P, NB * ST])
        rstd = sb("rstd", [P, NB * ST])
        y = sb("y", [P, 2, NB, ST, D])
        emb, biasR = gn[0:NSTAGE, 0, 0, :], gn[0:B, 0, 1, :]
        zeros = farT[:, 0, 0:S]
        once = prod[:, :, :, :].rearrange("p i t n -> p (i t n)")
        raw = once[:, 0:WC]
        rev = once[:, WC:WC + S + P]
        before = once[:, WC + S + P:WC + S + 3 * P].rearrange("p (m s) -> p m s", s=P)
        w4 = once[:, WC + S + 3 * P:WC + S + 3 * P + CT * P].rearrange("p (t r n) -> p t r n", r=REP, n=NT)
        blT = once[:, WC + S + 3 * P + CT * P:WC + S + 3 * P + CT * P + CT * NT].rearrange("p (t n) -> p t n", n=NT)
        powers = y[:, 1].rearrange("p b t d -> p (b t d)")[:, D:D + S + 1]
        nearP = [ctx.enter_context(nc.psum_tensor(f"nearP{i}", [P, CT, N], F32)) for i in range(2)]
        work = [ctx.enter_context(nc.psum_tensor(f"work{i}", [P, 2, N], F32)) for i in range(2)]

        stage_in, cols_in, blend_in, rows_in, wn2_in, w_in = (
            sem(n) for n in ("stage_in", "cols_in", "blend_in", "rows_in", "wn2_in", "w_in"))
        bias_out = sem("bias_out")
        x_in = sem("x_in")
        k_in = sem("k_in")
        xT_in = sem("xT_in")
        kT_in = sem("kT_in")
        bias_in = sem("bias_in")
        y_out = [sem(f"y_out{i}") for i in range(2)]
        c_zero, c_zeros = sem("c_zero"), sem("c_zeros")
        c_ident, c_row = sem("c_ident"), sem("c_row")
        c_exp, c_blexp = sem("c_exp"), sem("c_blexp")
        c_bias_ps, c_wrep_ps, c_leave_ps = sem("c_bias_ps"), sem("c_wrep_ps"), sem("c_leave_ps")
        c_hot, c_blmax, c_w4 = sem("c_hot"), sem("c_blmax"), sem("c_w4")
        c_biasrow, c_first_ps, c_first = sem("c_biasrow"), sem("c_first_ps"), sem("c_first")
        c_before, c_leave = sem("c_before"), sem("c_leave")
        c_whi, c_const, c_near = sem("c_whi"), sem("c_const"), sem("c_near")
        c_wrep, c_nearhi = sem("c_wrep"), sem("c_nearhi")
        c_dve = sem("c_dve")
        q_pool = sem("q_pool")
        qh_sb, ql_dv, kTh_sb, kTl_pool = sem("qh_sb"), sem("ql_dv"), sem("kTh_sb"), sem("kTl_pool")
        score_ps = sem("score_ps")
        max_dv, negmax_dv = sem("max_dv"), sem("negmax_dv")
        prob_sb = sem("prob_sb")
        rowinv_dv = sem("rowinv_dv")
        pT_ps, pT_sb, pTl_dv = sem("pT_ps"), sem("pT_sb"), sem("pTl_dv")
        knh_sb, knl_pool = sem("knh_sb"), sem("knl_pool")
        att_ps = sem("att_ps")
        x2_dv = sem("x2_dv")
        x2b_pool = sem("x2b_pool")
        x2T_ps, x2T_sb = sem("x2T_ps"), sem("x2T_sb")
        x2l_dv = sem("x2l_dv")
        cx_dv, cxh_sb, cxl_dv = sem("cx_dv"), sem("cxh_sb"), sem("cxl_dv")
        h1_ps, h1_sb = sem("h1_ps"), sem("h1_sb")
        g_ps, thG_sb, g_dv = sem("g_ps"), sem("thG_sb"), sem("g_dv")
        m_ps, thM_sb, ms_dv = sem("m_ps"), sem("thM_sb"), sem("ms_dv")
        mN_ps, mN_sb = sem("mN_ps"), sem("mN_sb")
        lv_pool = sem("lv_pool")
        gn_ps, gn_sb = sem("gn_ps"), sem("gn_sb")
        st_ps, Hw_dv = sem("st_ps"), sem("Hw_dv")
        farN_ps, farN_sb = sem("farN_ps"), sem("farN_sb")
        far_ps, far_sb = sem("far_ps"), sem("far_sb")
        near_ps, near_dv, near_pool = sem("near_ps"), sem("near_dv"), sem("near_pool")
        far_pool = sem("far_pool")
        half_dv = sem("half_dv")
        soma_ps, soma_sb = sem("soma_ps"), sem("soma_sb")
        acch_sb, accl_dv = sem("acch_sb"), sem("accl_dv")
        tg_ps, tg_sb, sg_dv = sem("tg_ps"), sem("tg_sb"), sem("sg_dv")
        sgh_sb, sgl_dv = sem("sgh_sb"), sem("sgl_dv")
        o_ps, o_sb = sem("o_ps"), sem("o_sb")
        st_dv, both_dv, mean_dv, var_dv = sem("st_dv"), sem("both_dv"), sem("mean_dv"), sem("var_dv")
        rstd_pool = sem("rstd_pool")
        cen_dv, y_dv = sem("cen_dv"), sem("y_dv")

        def need(eng, s, value):
            if not isinstance(value, int) or value > 0:
                eng.wait_ge(s, value)

        def steps(eng, body):
            def peeled(s):
                body(s, s + 2 < PAIRS, s + 1 < PAIRS, 0 <= s < PAIRS, s >= 1, (s + 1) % 2, (s + 1) // 2)

            peeled(-1)
            peeled(0)
            with eng.Fori(0, (PAIRS - 4) // 2) as i:
                body(i * 2 + 1, True, True, True, True, 0, i + 1)
                body(i * 2 + 2, True, True, True, True, 1, i + 1)
            for s in range(PAIRS - 3, PAIRS + 1):
                peeled(s)

        block = ctx.enter_context(nc.Block())

        @block.sync
        def _(sp):
            def load_xT(pair):
                sp.dma_start(xT[:, :, :, :], x_chn[pair]).then_inc(xT_in, 16)

            def load_bias(pair):
                sp.dma_start(bias[:, :, :], bias_d[pair].partition_broadcast(P)).then_inc(bias_in, 16)

            def load_kT(pair):
                sp.dma_start(kT[:, :, :, :], f_chn[pair]).then_inc(kT_in, 16)

            def load_kn(pair):
                sp.dma_start(kn[:, :, :, :], f_pos[pair]).then_inc(k_in, 16)

            def load_xn(pair):
                sp.dma_start(xn[:, :, :, :], x_pos[pair]).then_inc(x_in, 16)

            sp.dma_start(stI[:, :], stage.partition_broadcast(NSTAGE)).then_inc(stage_in, 16)
            sp.dma_start(emb, embed).then_inc(stage_in, 16)
            sp.dma_start(cols[:, :], columns).then_inc(cols_in, 16)
            load_xT(0)
            load_kT(0)
            sp.dma_start(blT[:, :, :], blend).then_inc(blend_in, 16)
            sp.wait_ge(c_biasrow, 1)
            sp.dma_start(bias_d.rearrange("q b s -> (q b) s"), biasR).then_inc(bias_out, 16)
            load_kn(0)
            load_xn(0)
            sp.dma_start(raw, weights).then_inc(w_in, 16)
            sp.dma_start(Wn2[:, :], wn2).then_inc(wn2_in, 16)
            sp.dma_start(gamma_beta[:, :, :].rearrange("p r d -> p (r d)"), rows.partition_broadcast(P))\
              .then_inc(rows_in, 16)

            def load_next(s, first=False):
                need(sp, knl_pool, s + 2)
                load_kn(s + 2)
                if first:
                    sp.wait_ge(score_ps, 2)
                    sp.wait_ge(bias_out, 16)
                need(sp, ql_dv, s + 1)
                load_xT(s + 2)
                load_bias(s + 2)
                need(sp, kTl_pool, s + 1)
                load_kT(s + 2)
                need(sp, x2_dv, (s + 2) * 4)
                load_xn(s + 2)

            def store_last(s, par):
                need(sp, y_dv, s * 4)
                sp.dma_start(out[s - 1], y[:, par]).then_inc(y_out[par], 16)

            load_next(-1, first=True)
            load_next(0)
            with sp.Fori(0, (PAIRS - 4) // 2) as i:
                for u in range(2):
                    load_next(i * 2 + 1 + u)
                    store_last(i * 2 + 1 + u, u)
            load_next(PAIRS - 3)
            for s in range(PAIRS - 3, PAIRS + 1):
                store_last(s, (s + 1) % 2)
            for par in range(2):
                sp.wait_ge(y_out[par], 16 * (PAIRS // 2 + 1))

        @block.gpsimd
        def _(pool):
            pool.memset(ident[:, :], 0.0).then_inc(c_zero, 1)
            pool.iota(rowI[:, :], pattern=[[0, 1]], base=0, channel_multiplier=1).then_inc(c_row, 1)
            pool.memset(zeros, 0.0).then_inc(c_zeros, 1)
            pool.memset(read[:, :, :, :], 0.0).then_inc(c_zeros, 1)
            pool.memset(carry[:, :], 0.0).then_inc(c_zeros, 1)
            pool.wait_ge(c_zero, 1)
            pool.affine_select(out=ident[:, :], in_=ident[:, :], compare_op=ALU.not_equal, fill=1.0, base=0,
                               pattern=[[-1, P]], channel_multiplier=1).then_inc(c_ident, 1)
            pool.memset(negHalf[:, :], -0.5).then_inc(c_zero, 1)
            pool.wait_ge(c_zero, 2)

            def queries(pair):
                need(pool, xT_in, (pair + 1) * 16)
                need(pool, bias_in, pair * 16)
                pool.tensor_tensor(qT[:, :, :, :], xT[:, :, :, :],
                                   bias[:, :, :].unsqueeze(1).to_broadcast([P, CT, NB, S]),
                                   ALU.add).then_inc(q_pool, 1)

            def keys_low_by_channel(pair):
                need(pool, kTh_sb, pair)
                pool.tensor_tensor(kTl[:, :, :, :], kT[:, :, :, :], kTh[:, :, :, :].bitcast(F32),
                                   ALU.subtract).then_inc(kTl_pool, 1)

            def keys_low(pair):
                need(pool, knh_sb, pair + 1)
                pool.tensor_tensor(knl[:, :, :, :], kn[:, :, :, :], knh[:, :, :, :].bitcast(F32),
                                   ALU.subtract).then_inc(knl_pool, 1)

            pool.wait_ge(c_first, 1)
            queries(0)
            keys_low(0)

            def body(s, n, a, r, z, pa, h):
                pr = 1 - pa

                def add(j):
                    if not r:
                        return
                    need(pool, near_dv, s * CH + j + 1)
                    if j == FAR_AFTER + 1:
                        need(pool, far_pool, s + 1)
                    elif j > 1:
                        need(pool, near_pool, s * NADD + j - 1)
                    T = CT if a else CT // 2
                    d = acc[:, pr, 0:T].rearrange("p t (c k) -> p t c k", k=CH)[:, :, :, j:CH]
                    src = prod[:, j % NPROD, 0:T, 0:CHN * (CH - j)].rearrange("p t (c k) -> p t c k", k=CH - j)
                    pool.tensor_tensor(d, d, src, ALU.add).then_inc(near_pool, 1)
                    if j == FAR_AFTER:
                        need(pool, far_sb, (s + 1) * 2)
                        need(pool, near_pool, s * NADD + j)
                        pool.tensor_tensor(acc[:, pr, 0:T], acc[:, pr, 0:T], farT[:, 0:T, :], ALU.add)\
                            .then_inc(far_pool, 1)

                for j in range(1, 4):
                    add(j)
                if n:
                    queries(s + 2)
                add(4)
                add(5)
                if n:
                    keys_low_by_channel(s + 2)
                    keys_low(s + 2)
                add(6)
                if z:
                    need(pool, var_dv, s)
                    pool.tensor_tensor(rstd[:, :], varE[:, :], negHalf[:, :], ALU.pow).then_inc(rstd_pool, 1)
                for j in range(7, CH):
                    add(j)
                if a:
                    if not r:
                        pool.wait_ge(c_leave, 1)
                    need(pool, mN_sb, s + 2)
                    if r:
                        need(pool, st_ps, (s + 1) * 4)
                    each = [P, NB * ST, CS, NT]
                    pool.tensor_tensor(lv[:, :, :, :], mN[:, :, :].unsqueeze(2).to_broadcast(each),
                                       leave[:, :, :].unsqueeze(1).to_broadcast(each),
                                       ALU.mult).then_inc(lv_pool, 1)
                    if not r:
                        pool.wait_ge(rows_in, 16)
                    need(pool, x2_dv, (s + 2) * 4)
                    if z:
                        need(pool, y_dv, s * 4)
                    pool.tensor_tensor(x2b[:, pa].rearrange("p b t d -> p (b t) d"),
                                       x2n[:, :, :, :].rearrange("p b t d -> p (b t) d"),
                                       betaB.unsqueeze(1).to_broadcast([P, NB * ST, D]),
                                       ALU.add).then_inc(x2b_pool, 1)

            steps(pool, body)

        @block.scalar
        def _(act):
            act.wait_ge(cols_in, 16)
            act.activation(alphaC[:, :], tauC, ACT.Exp).then_inc(c_exp, 1)
            act.activation(alphaX[:, :], tauX, ACT.Exp).then_inc(c_exp, 1)
            act.wait_ge(c_first_ps, 1)
            act.copy(bias[:, :, :].rearrange("p b s -> p (b s)"), work[0][:, 1, :]).then_inc(c_first, 1)
            act.wait_ge(c_blmax, 1)
            for t in range(CT):
                act.activation(blT[:, t, :], blT[:, t, :], ACT.Exp, bias=blM[:, t:t + 1],
                               accum_out=blS[:, t:t + 1]).then_inc(c_blexp, 1)

            def keys_high_by_channel(pair):
                need(act, kT_in, (pair + 1) * 16)
                need(act, score_ps, pair * 2)
                act.copy(kTh[:, :, :, :], kT[:, :, :, :]).then_inc(kTh_sb, 1)

            def keys_high(pair):
                need(act, k_in, (pair + 1) * 16)
                need(act, att_ps, pair * 2)
                act.copy(knh[:, :, :, :], kn[:, :, :, :]).then_inc(knh_sb, 1)

            keys_high(0)

            def body(s, n, a, r, z, pa, h):
                pr = 1 - pa

                def exps(b):
                    if a:
                        need(act, negmax_dv, (s + 1) * 2 + b + 1)
                        if b == 0 and r:
                            need(act, rowinv_dv, s + 1)
                        for t in range(ST):
                            act.activation(prob[:, b, t, :], work[0][:, b, t * S:(t + 1) * S], ACT.Exp,
                                           bias=negmax[:, b, t:t + 1],
                                           accum_out=rowsum[:, b, t:t + 1]).then_inc(prob_sb, 1)

                exps(0)
                if r:
                    for b in range(NB):
                        need(act, gn_ps, s * 2 + b + 1)
                        act.copy(gn[:, b].rearrange("p t d -> p (t d)"), work[1][:, b, :]).then_inc(gn_sb, 1)
                exps(1)
                if z:
                    need(act, near_pool, s * NADD)
                    if not r:
                        act.wait_ge(half_dv, NADD)
                    for t in range(CT):
                        act.copy(tailh[:, t, :], acc[:, pa, t, :]).then_inc(acch_sb, 1)
                if r:
                    for t in range(CT):
                        need(act, soma_ps, s * 2 + t + 1)
                        act.activation(soma[:, pr, t, :], work[1][:, t, :], ACT.Gelu,
                                       bias=bsC[:, t:t + 1]).then_inc(soma_sb, 1)
                if a:
                    for t in range(ST):
                        need(act, pT_ps, (s + 1) * 2 + t + 1)
                        act.copy(probTh[:, t].rearrange("p b s -> p (b s)"), work[0][:, t, :]).then_inc(pT_sb, 1)
                if a and not r:
                    act.wait_ge(w_in, 16)
                    act.copy(WH[:, :], raw).then_inc(c_whi, 1)
                    act.wait_ge(c_wrep, 1)
                    for j in range(CH):
                        act.activation(near[:, j, :], wrep[:, :], ACT.Copy, scale=powers[:, j:j + 1])\
                           .then_inc(c_nearhi, 1)
                    act.wait_ge(c_const, 2)
                if z:
                    for t in range(CT):
                        need(act, tg_ps, (s - 1) * 2 + t + 1)
                        if t == 0 and r:
                            need(act, g_dv, (s + 1) * 2)
                        act.activation(th[:, t, :], work[1][:, t, :], ACT.Tanh, bias=btC[:, t:t + 1],
                                       scale=0.5).then_inc(tg_sb, 1)
                    for t in range(CT):
                        need(act, sg_dv, (s - 1) * 2 + t + 1)
                        act.copy(tailh[:, t, :], th[:, t, :]).then_inc(sgh_sb, 1)
                if n:
                    keys_high_by_channel(s + 2)
                    keys_high(s + 2)
                if a:
                    for t in range(CT):
                        need(act, x2T_ps, (s + 1) * 2 + t + 1)
                        act.copy(x2h[:, t].rearrange("p b s -> p (b s)"), work[0][:, t, :])
                        act.copy(x2T[:, t].rearrange("p b s -> p (b s)"), work[0][:, t, :]).then_inc(x2T_sb, 1)
                if z:
                    for b in range(NB):
                        need(act, o_ps, (s - 1) * 2 + b + 1)
                        if b == 0:
                            need(act, y_out[pa], h * 16)
                        act.copy(y[:, pa, b].rearrange("p t d -> p (t d)"),
                                 work[1][:, b, :]).then_inc(o_sb, 1)
                if n:
                    need(act, q_pool, s + 3)
                    act.copy(qh, qT[:, :, :, :]).then_inc(qh_sb, 1)
                if r:
                    for t in range(ST):
                        need(act, farN_ps, s * 2 + t + 1)
                        act.copy(farN[:, t].rearrange("p b d -> p (b d)"), work[1][:, t, :]).then_inc(farN_sb, 1)
                    for t in range(CT):
                        need(act, far_ps, s * 2 + t + 1)
                        if t == 0:
                            need(act, far_pool, s)
                        act.copy(farT[:, t, :], work[1][:, t, :]).then_inc(far_sb, 1)
                if a:
                    for k in range(CT):
                        need(act, cx_dv, (s + 1) * 4 + (k + 1) * NB)
                        act.copy(cxh[:, k, :, :], cxT[:, k, :, :]).then_inc(cxh_sb, 1)
                if a:
                    need(act, h1_ps, s + 2)
                    act.activation(h1, work[0][:, 0, :], ACT.Gelu, bias=bn1C).then_inc(h1_sb, 1)
                    for t in range(CT):
                        need(act, g_ps, (s + 1) * 2 + t + 1)
                        if t == 0 and z:
                            need(act, sgl_dv, s * 2)
                        act.activation(th[:, t, :], work[1][:, t, :], ACT.Tanh, bias=bgC[:, t:t + 1],
                                       scale=0.5).then_inc(thG_sb, 1)
                        if t == 0:
                            need(act, m_ps, s + 2)
                            act.activation(thM, work[0][:, 0, :], ACT.Tanh, bias=bn2C,
                                           scale=0.5).then_inc(thM_sb, 1)
                    need(act, mN_ps, s + 2)
                    if r:
                        need(act, lv_pool, s + 1)
                    act.activation(mN[:, :, :], work[0][:, 1, :].rearrange("p (q n) -> p q n", n=P)[:, :, 0:NT],
                                   ACT.Copy, bias=2.0).then_inc(mN_sb, 1)

            steps(act, body)

        @block.tensor
        def _(pe):
            pe.wait_ge(c_hot, 1)
            pe.matmul(work[0][0:B, 0, 0:S], hot[:, :], emb, start=True, stop=True).then_inc(c_bias_ps, 1)
            for b in range(NB):
                ins = pe.matmul(work[0][:, 1, b * S:(b + 1) * S], hot[:, b:b + 1].to_broadcast([NSTAGE, P]), emb,
                                start=True, stop=True)
            ins.then_inc(c_first_ps, 1)

            def transposes(dst, src_of, done, free=lambda t: None):
                for t in range(2):
                    free(t)
                    for i in range(N // P):
                        ins = pe.transpose(dst[:, t, i * P:(i + 1) * P], src_of(t, i), ident[:, :])
                    ins.then_inc(done, 1)

            def thrice(dst, l, r, first, last):
                pe.matmul(dst, l[0], r[0], start=first, stop=False)
                pe.matmul(dst, l[1], r[0], start=False, stop=False)
                return pe.matmul(dst, l[0], r[1], start=False, stop=last)

            def blocks(w, k, e):
                return [v[:, k, e * P:(e + 1) * P] for v in w]

            def flat(hi, lo, k):
                return [v[:, k].rearrange("p b s -> p (b s)") for v in (hi, lo)]

            def body(s, n, a, r, z, pa, h):
                pr = 1 - pa

                def near_group(g):
                    if not r:
                        return
                    p = nearP[g % 2]
                    if g == 0:
                        need(pe, ms_dv, (s + 1) * 2)
                    if not z:
                        pe.wait_ge(c_near, (GROUPS[g][-1] + 1) * REP // 2)
                    last = GROUPS[g - 2][-1] + 1 if g >= 2 else GROUPS[NG - 2 + g][-1] + 1 - CH
                    need(pe, near_dv, s * CH + last)
                    for t in range(CT):
                        at = 0
                        for j in GROUPS[g]:
                            k = width(j)
                            ins = pe.matmul(p[:, t, at:at + CHN * k], near[:, j, t * P:(t + 1) * P],
                                            ms[:, pr, :].rearrange("p (c k) -> p c k", k=CH)[:, :, 0:k],
                                            start=True, stop=True)
                            at += CHN * k
                    ins.then_inc(near_ps, 1)

                def states(b, free):
                    for m in range(KT):
                        if m % 2 == 0:
                            free(m // 2)
                        at = m * REP % CS
                        ins = pe.matmul(work[1][:, m // 2, (m % 2) * D:(m % 2 + 1) * D],
                                        lv[:, b * ST + m * REP // CS, at:at + REP, :].rearrange("p c n -> p (c n)"),
                                        gn[:, b, m * REP // CS, :], start=True, stop=True)
                        if m % 2:
                            ins.then_inc(st_ps, 1)

                if a:
                    if r:
                        need(pe, ql_dv, s + 1)
                        need(pe, kTl_pool, s + 1)
                    else:
                        pe.wait_ge(c_biasrow, 1)
                        pe.wait_ge(q_pool, 1)
                        pe.wait_ge(kT_in, 16)
                    for b in range(NB):
                        if r:
                            need(pe, mN_sb if b else thM_sb, s + 1)
                        for t in range(ST):
                            out, at = work[0][:, b, t * S:(t + 1) * S], slice(t * P, (t + 1) * P)
                            for k in range(CT):
                                if r:
                                    ins = thrice(out, [v[:, k, b, at] for v in (qh, ql)],
                                                 [v[:, k, b, :] for v in (kTh, kTl)], k == 0, k == CT - 1)
                                else:
                                    ins = pe.matmul(out, qT[:, k, b, at], kT[:, k, b, :],
                                                    start=(k == 0), stop=(k == CT - 1))
                        ins.then_inc(score_ps, 1)
                if a and not r:
                    pe.wait_ge(c_ident, 1)
                    pe.wait_ge(c_before, 1)
                    for m in range(CS // REP):
                        ins = pe.transpose(work[1][:, 1, m * P:(m + 1) * P], before[:, m, :], ident[:, :])
                    ins.then_inc(c_leave_ps, 1)
                    pe.wait_ge(c_w4, 1)
                    for t in range(CT):
                        ins = pe.transpose(work[1][:, 0, t * P:(t + 1) * P],
                                           w4[:, t].rearrange("p r n -> p (r n)"), ident[:, :])
                    ins.then_inc(c_wrep_ps, 1)
                if r:
                    need(pe, g_dv, (s + 1) * 2)
                    transposes(work[1], lambda b, i: gT[:, pr, i % CT, b * S + i // CT * P:b * S + (i // CT + 1) * P],
                               gn_ps, lambda b: need(pe, thG_sb, s * 2 + b + 1))
                near_group(0)
                near_group(1)
                if r:
                    for e in range(CT):
                        need(pe, gn_sb, s * 2 + e + 1)
                        for k in range(CT):
                            ins = thrice(work[1][:, e, :], blocks(Ws, k, e), flat(x2h, x2l, k), k == 0, k == CT - 1)
                        ins.then_inc(soma_ps, 1)
                if a:
                    need(pe, prob_sb, (s + 2) * 4)
                    transposes(work[0], lambda t, i: prob[:, i // ST, i % ST, t * P:(t + 1) * P], pT_ps)
                near_group(2)
                if z:
                    need(pe, accl_dv, s * 2)
                    if not r:
                        need(pe, o_sb, (s - 1) * 2)
                    for e in range(CT):
                        if r:
                            need(pe, soma_sb, s * 2 + e + 1)
                        for k in range(CT):
                            ins = thrice(work[1][:, e, :], blocks(Wt, k, e), (tailh[:, k, :], taill[:, k, :]),
                                         k == 0, k == CT - 1)
                        ins.then_inc(tg_ps, 1)
                near_group(3)
                if a:
                    need(pe, pTl_dv, (s + 2) * 2)
                    need(pe, knl_pool, s + 2)
                    for b in range(NB):
                        for t in range(ST):
                            for k in range(ST):
                                ins = thrice(work[0][:, b, t * D:(t + 1) * D],
                                             [v[:, k, b, t * P:(t + 1) * P] for v in (probTh, probTl)],
                                             [v[:, b, k, :] for v in (knh, knl)], k == 0, k == ST - 1)
                        ins.then_inc(att_ps, 1)
                near_group(4)
                if r:
                    need(pe, lv_pool, s + 1)
                    need(pe, gn_sb, (s + 1) * 2)
                    states(0, lambda k: z and need(pe, tg_sb, (s - 1) * 2 + k + 1))
                near_group(5)
                if a:
                    need(pe, x2_dv, (s + 2) * 4)
                    transposes(work[0], lambda t, i: x2n[:, i // ST, i % ST, t * P:(t + 1) * P], x2T_ps)
                if z:
                    need(pe, sgl_dv, s * 2)
                    for b in range(NB):
                        if r:
                            need(pe, Hw_dv, s * 4 + b + 1)
                        for t in range(ST):
                            at = slice(b * S + t * P, b * S + (t + 1) * P)
                            for k in range(CT):
                                ins = thrice(work[1][:, b, t * D:(t + 1) * D], (tailh[:, k, at], taill[:, k, at]),
                                             [w[:, k, :] for w in Wo], k == 0, k == CT - 1)
                        ins.then_inc(o_ps, 1)
                if r:
                    states(1, lambda k: need(pe, o_sb, (s - 1) * 2 + k + 1) if z else need(pe, Hw_dv, s * 4 + k + 1))
                near_group(6)
                near_group(7)
                if r:
                    for m in range(KT):
                        at, t = m * REP * CH % P, m * REP * CH // P
                        if at == 0:
                            need(pe, Hw_dv, s * 4 + 2 + t + 1)
                        out = work[1][at:at + REP * CH, t, :]
                        ins = pe.matmul(out, read[:, int(at > 0)].rearrange("p c k -> p (c k)"),
                                        Hw[:, m, :, :].rearrange("p b d -> p (b d)"), start=True, stop=(t == 0))
                        if t:
                            ins = pe.matmul(out, carry[:, at:at + REP * CH],
                                            Hw[:, 0, :, :].rearrange("p b d -> p (b d)"), start=False, stop=True)
                        if at + REP * CH == P:
                            ins.then_inc(farN_ps, 1)
                near_group(8)
                if r:
                    need(pe, farN_sb, (s + 1) * 2)
                    transposes(work[1], lambda t, i: farN[:, i % ST, i // ST, t * P:(t + 1) * P], far_ps)
                if a:
                    if not r:
                        pe.wait_ge(c_const, 2)
                        pe.wait_ge(wn2_in, 16)
                    need(pe, x2T_sb, (s + 2) * 2)
                    need(pe, x2l_dv, (s + 2) * 2)
                    for k in range(CT):
                        ins = thrice(work[0][:, 0, :], [w[:, k, :] for w in Wn1], flat(x2h, x2l, k),
                                     k == 0, k == CT - 1)
                    ins.then_inc(h1_ps, 1)
                if a:
                    for e in range(CT):
                        if r:
                            need(pe, far_sb, s * 2 + e + 1)
                        for k in range(CT):
                            thrice(work[1][:, e, :], blocks(Wg, k, e), flat(x2h, x2l, k), k == 0, False)
                near_group(9)
                if a:
                    need(pe, cxl_dv, (s + 2) * 2)
                    for e in range(CT):
                        for k in range(CT):
                            ins = thrice(work[1][:, e, :], blocks(Wg, CT + k, e), flat(cxh, cxl, k),
                                         False, k == CT - 1)
                        ins.then_inc(g_ps, 1)
                        if e == 0:
                            need(pe, h1_sb, s + 2)
                            pe.matmul(work[0][:, 0, :], Wn2[:, :], h1, start=True, stop=True)\
                              .then_inc(m_ps, 1)
                if a:
                    need(pe, thM_sb, s + 2)
                    for i in range(N // P):
                        ins = pe.transpose(work[0][:, 1, i * P:(i + 1) * P], thM[:, i * P:(i + 1) * P],
                                           ident[:, :])
                    ins.then_inc(mN_ps, 1)
                near_group(10)
                near_group(11)

            steps(pe, body)

        @block.vector
        def _(dve):
            chain = [0]

            def link(ins):
                chain[0] += 1
                ins.then_inc(c_dve, 1)
                dve.wait_ge(c_dve, chain[0])

            dve.wait_ge(stage_in, 32)
            dve.wait_ge(c_row, 1)
            link(dve.tensor_copy(stF[:, :], stI[:, :]))
            link(dve.tensor_copy(rowF[:, :], rowI[:, :]))
            dve.tensor_scalar(hot[:, :], stF[:, :], rowF[:, 0:1], None, ALU.is_equal).then_inc(c_hot, 1)
            dve.wait_ge(c_exp, 2)
            for a_ in (alphaC, alphaX):
                link(dve.tensor_scalar(a_[:, :], a_[:, :], 1.0, None, ALU.add))
                link(dve.reciprocal(a_[:, :], a_[:, :]))
            dve.wait_ge(c_bias_ps, 1)
            dve.tensor_copy(biasR, work[0][0:B, 0, 0:S]).then_inc(c_biasrow, 1)
            dve.wait_ge(c_zeros, 3)
            dve.memset(powers[:, 0:1], 1.0)
            link(dve.tensor_tensor_scan(powers[:, 1:S + 1], alphaC[:, 0:1].to_broadcast([P, S]), zeros,
                                        1.0, ALU.mult, ALU.add))
            dve.memset(rev[:, S:], 0.0)
            link(dve.tensor_copy(rev[:, 0:S], powers[:, 0:S][:, ::-1]))
            for c in range(CS):
                part, m, start = slice(c % REP * NT, (c % REP + 1) * NT), c // REP, c * CH or P
                ins = dve.tensor_copy(before[part, m, :], rev[part, S - start:S - start + P])
            ins.then_inc(c_before, 1)
            dve.wait_ge(blend_in, 16)
            link(dve.tensor_reduce(blM[:, :], blT[:, :, :], AX_X, ALU.max))
            dve.tensor_scalar(blM[:, :], blM[:, :], -1.0, None, ALU.mult).then_inc(c_blmax, 1)
            for r in range(REP):
                for i in range(2):
                    if r + i > 0:
                        dve.tensor_copy(read[r * NT:(r + 1) * NT, i, r, :], powers[r * NT:(r + 1) * NT, 1:1 + CH])
            dve.tensor_copy(carry[0:NT, :], powers[0:NT, 1:1 + P])
            for v in (bgC, btC, bn2C):
                dve.tensor_scalar(v, v, 0.5, None, ALU.mult)
            dve.wait_ge(c_blexp, CT)
            link(dve.reciprocal(blR[:, :], blS[:, :]))
            for t in range(CT):
                for r in range(REP):
                    ins = dve.tensor_scalar(w4[:, t, r, :], blT[:, t, :], blR[:, t:t + 1], 0.25,
                                            ALU.mult, ALU.mult)
            ins.then_inc(c_w4, 1)
            for par in range(2):
                dve.memset(y[:, par, 0, 0, 0:1], 0.0).then_inc(y_out[par], 16)

            def near_weights(js):
                for j in js:
                    dve.wait_ge(c_nearhi, j + 1)
                    for r in range(1, REP, 2):
                        part = slice(r * NT, (r + 1) * NT)
                        dve.scalar_tensor_tensor(out=near[part, j, :], in0=wrep[part, :],
                                                 scalar=powers[part, j:j + 1], in1=near[part, j, :].bitcast(F32),
                                                 op0=ALU.mult, op1=ALU.subtract).then_inc(c_near, 1)

            def body(s, n, a, r, z, pa, h):
                def near_group(g, pair, par, on, halves):
                    if not on:
                        return
                    if g == 0 and not a:
                        need(dve, g_dv, (pair + 1) * 2)
                    need(dve, near_ps, pair * NG + g + 1)
                    at = 0
                    for j in GROUPS[g]:
                        n, m = width(j), CH - j
                        src = nearP[g % 2][:, :, at:at + CHN * n].rearrange("p t (c k) -> p t c k", k=n)
                        gv = gT[:, par].rearrange("p t (c k) -> p t c k", k=CH)
                        dst = prod[:, j % NPROD, :, 0:CHN * m].rearrange("p t (c k) -> p t c k", k=m)
                        if j == 0:
                            dst = acc[:, par].rearrange("p t (c k) -> p t c k", k=CH)
                        else:
                            need(dve, near_pool, pair * NADD + (j - NPROD if j >= NPROD else j - NPROD + 1))
                        dve.tensor_tensor(dst, src[:, :, :, 0:m], gv[:, :, :, 0:m], ALU.mult)\
                           .then_inc(near_dv, 1)
                        at += CHN * n
                        if halves and j > 0:
                            T = CT // 2
                            need(dve, near_dv, pair * CH + j + 1)
                            d = acc[:, par, T:].rearrange("p t (c k) -> p t c k", k=CH)[:, :, :, j:]
                            dve.tensor_tensor(d, d, dst[:, T:], ALU.add).then_inc(half_dv, 1)
                            if j == FAR_AFTER:
                                need(dve, far_sb, (pair + 1) * 2)
                                dve.wait_ge(half_dv, j)
                                dve.tensor_tensor(acc[:, par, T:], acc[:, par, T:], farT[:, T:, :], ALU.add)

                def gate(t):
                    need(dve, thG_sb, (s + 1) * 2 + t + 1)
                    if t == 0 and r:
                        need(dve, gn_ps, s * 2)
                    dve.scalar_tensor_tensor(out=gT[:, pa, t, :], in0=th[:, t, :], scalar=1.0,
                                             in1=x2T[:, t].rearrange("p b s -> p (b s)"),
                                             op0=ALU.add, op1=ALU.mult).then_inc(g_dv, 1)

                def weigh_states(b):
                    for k in range(2):
                        need(dve, st_ps, s * 4 + 2 * b + k + 1)
                        dve.tensor_tensor(
                            Hw[:, 2 * k:2 * k + 2, b, :],
                            work[1][:, k, :].rearrange("p (m d) -> p m d", d=D),
                            wrep[:, :].unsqueeze(1).to_broadcast([P, 2, D]), ALU.mult).then_inc(Hw_dv, 1)

                for b in range(NB):
                    if a:
                        need(dve, score_ps, (s + 1) * 2 + b + 1)
                        dve.tensor_reduce(rowmax[:, b, :], work[0][:, b, :].rearrange("p (t s) -> p t s", s=S),
                                          AX_X, ALU.max).then_inc(max_dv, 1)
                        need(dve, max_dv, (s + 1) * 2 + b + 1)
                        dve.tensor_scalar(negmax[:, b, :], rowmax[:, b, :], -1.0, None, ALU.mult)\
                           .then_inc(negmax_dv, 1)
                    if b == 0:
                        near_group(NG - 1, s - 1, pa, z, not r)
                if a and not r:
                    dve.wait_ge(c_leave_ps, 1)
                    dve.tensor_copy(leave[:, :, :], work[1][:, 1, 0:CS * NT].rearrange("p (c n) -> p c n", n=NT))\
                       .then_inc(c_leave, 1)
                    dve.wait_ge(c_wrep_ps, 1)
                    dve.tensor_copy(wrep[:, :], work[1][:, 0, 0:D]).then_inc(c_wrep, 1)
                near_group(0, s, 1 - pa, r, not a)
                near_group(1, s, 1 - pa, r, not a)
                if r and not z:
                    near_weights(range(8, 10))
                if z:
                    for t in range(CT):
                        need(dve, acch_sb, (s - 1) * 2 + t + 1)
                        dve.tensor_tensor(taill[:, t, :], acc[:, pa, t, :], tailh[:, t, :].bitcast(F32),
                                          ALU.subtract).then_inc(accl_dv, 1)
                near_group(2, s, 1 - pa, r, not a)
                if a:
                    need(dve, prob_sb, (s + 2) * 4)
                    dve.reciprocal(rowinv[:, :, :], rowsum[:, :, :]).then_inc(rowinv_dv, 1)
                    for t in range(ST):
                        need(dve, pT_sb, (s + 1) * 2 + t + 1)
                        dve.tensor_tensor(probTl[:, t].rearrange("p b s -> p (b s)"), work[0][:, t, :],
                                          probTh[:, t].rearrange("p b s -> p (b s)").bitcast(F32),
                                          ALU.subtract).then_inc(pTl_dv, 1)
                    if not r:
                        dve.wait_ge(c_whi, 1)
                        link(dve.tensor_tensor(WL[:, :], raw, WH[:, :].bitcast(F32), ALU.subtract))
                        for w in Wo:
                            dve.tensor_scalar(w[:, :, :], w[:, :, :].bitcast(F32), 0.5, None, ALU.mult)\
                               .then_inc(c_const, 1)
                if z:
                    for t in range(CT):
                        need(dve, tg_sb, (s - 1) * 2 + t + 1)
                        dve.scalar_tensor_tensor(out=th[:, t, :], in0=th[:, t, :], scalar=1.0,
                                                 in1=soma[:, pa, t, :], op0=ALU.add, op1=ALU.mult)\
                           .then_inc(sg_dv, 1)
                near_group(3, s, 1 - pa, r, not a)
                if r and not z:
                    near_weights(range(10, 12))
                if z:
                    for t in range(CT):
                        need(dve, sgh_sb, (s - 1) * 2 + t + 1)
                        dve.tensor_tensor(taill[:, t, :], th[:, t, :], tailh[:, t, :].bitcast(F32),
                                          ALU.subtract).then_inc(sgl_dv, 1)
                if a:
                    need(dve, rowinv_dv, s + 2)
                    need(dve, x_in, (s + 2) * 16)
                    if r:
                        need(dve, x2b_pool, s + 1)
                    for b in range(NB):
                        need(dve, att_ps, (s + 1) * 2 + b + 1)
                        for t in range(ST):
                            dve.scalar_tensor_tensor(
                                out=x2n[:, b, t, :], in0=work[0][:, b, t * D:(t + 1) * D],
                                scalar=rowinv[:, b, t:t + 1], in1=xn[:, b, t, :],
                                op0=ALU.mult, op1=ALU.add).then_inc(x2_dv, 1)
                if r:
                    weigh_states(0)
                near_group(4, s, 1 - pa, r, not a)
                near_group(5, s, 1 - pa, r, not a)
                if r and not z:
                    near_weights(range(12, 14))
                if a:
                    for k in range(CT):
                        need(dve, x2T_sb, (s + 1) * 2 + k + 1)
                        dve.tensor_tensor(x2l[:, k, :, :], x2T[:, k, :, :], x2h[:, k, :, :].bitcast(F32),
                                          ALU.subtract).then_inc(x2l_dv, 1)
                if z:
                    for b in range(NB):
                        need(dve, o_sb, (s - 1) * 2 + b + 1)
                        for t in range(ST):
                            dve.bn_stats(stats[:, b * ST + t, :], y[:, pa, b, t, :]).then_inc(st_dv, 1)
                if r:
                    weigh_states(1)
                near_group(6, s, 1 - pa, r, not a)
                if a:
                    for k in range(CT):
                        for b in range(NB):
                            dve.tensor_tensor_scan(cxT[:, k, b, :], alphaX[:, 0:1].to_broadcast([P, S]),
                                                   x2T[:, k, b, :], 0.0, ALU.mult, ALU.add).then_inc(cx_dv, 1)
                if not r and a:
                    near_weights(range(0, 3))
                if z:
                    need(dve, st_dv, s * 4)
                    dve.tensor_tensor(both[:, :, :], stats[:, :, 1:3], stats[:, :, 4:6], ALU.add)\
                       .then_inc(both_dv, 1)
                    dve.tensor_tensor(dif[:, :], stats[:, :, 1], stats[:, :, 4], ALU.subtract)\
                       .then_inc(both_dv, 1)
                    need(dve, both_dv, s * 2)
                    dve.tensor_scalar(mean[:, :], both[:, :, 0], 0.5, None, ALU.mult).then_inc(mean_dv, 1)
                    dve.tensor_tensor(dif2[:, :], dif[:, :], dif[:, :], ALU.mult).then_inc(mean_dv, 1)
                    dve.tensor_scalar(varE[:, :], both[:, :, 1], 1.0 / D, EPS, ALU.mult, ALU.add)\
                       .then_inc(mean_dv, 1)
                    need(dve, mean_dv, s * 3)
                    dve.scalar_tensor_tensor(out=varE[:, :], in0=dif2[:, :], scalar=0.25, in1=varE[:, :],
                                             op0=ALU.mult, op1=ALU.add).then_inc(var_dv, 1)
                near_group(7, s, 1 - pa, r, not a)
                if r and not z:
                    near_weights(range(14, CH))
                if n:
                    need(dve, qh_sb, s + 2)
                    dve.tensor_tensor(ql, qT[:, :, :, :], qh.bitcast(F32), ALU.subtract).then_inc(ql_dv, 1)
                if a:
                    for k in range(CT):
                        need(dve, cxh_sb, (s + 1) * 2 + k + 1)
                        dve.tensor_tensor(cxl[:, k, :, :], cxT[:, k, :, :], cxh[:, k, :, :].bitcast(F32),
                                          ALU.subtract).then_inc(cxl_dv, 1)
                if z:
                    for q in range(NB * ST):
                        v = y[:, pa, q // ST, q % ST, :]
                        dve.scalar_tensor_tensor(
                            out=v, in0=v, scalar=mean[:, q:q + 1],
                            in1=gammaB[:, :], op0=ALU.subtract, op1=ALU.mult).then_inc(cen_dv, 1)
                near_group(8, s, 1 - pa, r, not a)
                if not r and a:
                    near_weights(range(3, 6))
                if z:
                    need(dve, rstd_pool, s)
                    need(dve, x2b_pool, s)
                    need(dve, cen_dv, s * 4)
                    for q in range(NB * ST):
                        v = y[:, pa, q // ST, q % ST, :]
                        dve.scalar_tensor_tensor(
                            out=v, in0=v, scalar=rstd[:, q:q + 1],
                            in1=x2b[:, pa, q // ST, q % ST, :], op0=ALU.mult, op1=ALU.add).then_inc(y_dv, 1)
                near_group(9, s, 1 - pa, r, not a)
                if a:
                    gate(0)
                    need(dve, thM_sb, s + 2)
                    dve.tensor_scalar(ms[:, pa, :], thM, 2.0, None, ALU.add).then_inc(ms_dv, 1)
                    need(dve, ms_dv, (s + 1) * 2 + 1)
                    up = slice(P // 2, P)
                    dve.scalar_tensor_tensor(out=ms[up, pa, :], in0=thM[up, :], scalar=2.0,
                                             in1=ms[up, pa, :].bitcast(F32), op0=ALU.add, op1=ALU.subtract)\
                       .then_inc(ms_dv, 1)
                near_group(10, s, 1 - pa, r, not a)
                if not r and a:
                    near_weights(range(6, 8))
                if a:
                    gate(1)

            steps(dve, body)


def kernel(x, fside_BxSxS_0, itok_B_0_5, condB_tauraws, cond_256, condB_bn2, cond_1024, L0_cond_braak_embed,
           L1_cond_tau_ctx, L1_cond_Wg, L1_cond_bg, L1_cond_Wn1, L1_cond_bn1, L1_cond_Wsoma, L1_cond_bsoma,
           L1_cond_Wtemp, L1_cond_btemp, L1_cond_Wout, L1_cond_gamma, L1_cond_beta):
    import numpy as np
    import concourse.bacc as bacc
    from concourse.bass_utils import run_bass_kernel_spmd

    def by_partition(v):
        return np.asarray(v).reshape(-1, P).T

    B, S, D = x.shape
    NB = 2

    def by_position(v):
        return np.asarray(v).reshape(B // NB, NB, S // P, P, D).transpose(0, 3, 1, 2, 4)

    def by_channel(v):
        return np.asarray(v).reshape(B // NB, NB, S, D // P, P).transpose(0, 4, 3, 1, 2)

    def by_row(w):
        return w.reshape(-1, P, w.shape[1]).transpose(1, 0, 2).reshape(P, -1)

    def padded(v, *shape):
        v = np.asarray(v)
        out = np.zeros(shape, v.dtype)
        out[tuple(slice(0, n) for n in v.shape)] = v
        return out

    NT, NH = np.asarray(cond_256).shape
    copies = P // NT
    tau_ctx = np.broadcast_to(np.asarray(L1_cond_tau_ctx).reshape(1, 1), (P, 1))
    columns = [by_partition(L1_cond_bg), by_partition(L1_cond_bsoma), by_partition(L1_cond_btemp),
               padded(L1_cond_bn1, P)[:, None], np.tile(np.asarray(condB_bn2), copies)[:, None],
               np.tile(np.asarray(condB_tauraws), copies)[:, None], tau_ctx]
    weights = [np.asarray(w).T for w in (L1_cond_Wg, L1_cond_Wsoma, L1_cond_Wtemp, L1_cond_Wout)]
    weights.append(padded(np.asarray(L1_cond_Wn1).T, D, P))
    arrays = {
        "x_pos": by_position(x), "f_pos": by_position(fside_BxSxS_0),
        "x_chn": by_channel(x), "f_chn": by_channel(fside_BxSxS_0), "stage": itok_B_0_5,
        "embed": L0_cond_braak_embed,
        "blend": by_row(np.asarray(cond_1024).T).reshape(P, D // P, NT),
        "columns": np.concatenate(columns, axis=1),
        "rows": np.concatenate([np.asarray(L1_cond_gamma), np.asarray(L1_cond_beta)]),
        "wn2": padded(np.tile(np.asarray(cond_256).T, (1, copies)), P, P),
        "weights": np.concatenate([by_row(w) for w in weights], axis=1),
    }
    arrays = {"in_" + k: np.ascontiguousarray(v) for k, v in arrays.items()}
    nc = bacc.Bacc("TRN2", target_bir_lowering=False, num_devices=1)
    args = [nc.dram_tensor(k, v.shape, mybir.dt.from_np(v.dtype), kind="ExternalInput").ap()
            for k, v in arrays.items()]
    out = nc.dram_tensor("out", arrays["in_x_pos"].shape, F32, kind="ExternalOutput").ap()
    build(nc, *args, out)
    got = run_bass_kernel_spmd(nc, [arrays], core_ids=[0]).results[0]["out"]
    return got.transpose(0, 2, 3, 1, 4).reshape(B, S, D)
```
